# Optimizing a Trainium2 kernel written in Bass

```python
import numpy as np
import jax
import jax.numpy as jnp

def _softmax(x, axis=-1):
    return jax.nn.softmax(x, axis=axis)

def _gelu(x):
    return jax.nn.gelu(x, approximate=True)

def _silu(x):
    return jax.nn.silu(x)

def _sigmoid(x):
    return jax.nn.sigmoid(x)

def _layernorm(x, axis=-1, eps=1e-05):
    m = jnp.mean(x, axis=axis, keepdims=True)
    v = jnp.var(x, axis=axis, keepdims=True)
    return (x - m) / jnp.sqrt(v + eps)

def _scatter_add(tgt, idx, src, axis=0):
    return tgt.at[idx].add(src)

def _segment_sum(src, seg, n):
    return jax.ops.segment_sum(src, seg, n)
kernel_name = 'mk_conv_seq_d2_conv_nchw256_r2_99af2b'

def setup_inputs(seed: int=0):
    np.random.seed(seed)
    _w = jnp.asarray

    def _rec_inputs():
        import jax
        import jax.numpy as jnp
        _gk = jax.random.key(seed)
        x = -0.0003929 + 0.9999 * jax.random.normal(jax.random.fold_in(_gk, 1), (16, 128, 32, 32), jnp.float32)
        return x
    x = _rec_inputs()

    def _L0_conv_setup():
        import jax, jax.numpy as jnp
        from jax import lax
        import numpy as np
        S = 0.7071067811865476

        def dwt2(x):
            lo = (x[..., 0::2, :] + x[..., 1::2, :]) * S
            hi = (x[..., 0::2, :] - x[..., 1::2, :]) * S
            cA = (lo[..., 0::2] + lo[..., 1::2]) * S
            cV = (lo[..., 0::2] - lo[..., 1::2]) * S
            cH = (hi[..., 0::2] + hi[..., 1::2]) * S
            cD = (hi[..., 0::2] - hi[..., 1::2]) * S
            return (cA, cH, cV, cD)

        def _interleave(e, o, axis):
            s = jnp.stack([e, o], axis=axis)
            shp = list(e.shape)
            shp[axis] = shp[axis] * 2 if axis >= 0 else shp[axis] * 2
            out_shape = list(e.shape)
            out_shape[axis % e.ndim] *= 2
            return s.reshape(out_shape)

        def idwt2(cA, cH, cV, cD):
            lo_e = (cA + cV) * S
            lo_o = (cA - cV) * S
            lo = jnp.stack([lo_e, lo_o], axis=-1).reshape(cA.shape[:-1] + (cA.shape[-1] * 2,))
            hi_e = (cH + cD) * S
            hi_o = (cH - cD) * S
            hi = jnp.stack([hi_e, hi_o], axis=-1).reshape(cH.shape[:-1] + (cH.shape[-1] * 2,))
            r_e = (lo + hi) * S
            r_o = (lo - hi) * S
            B = lo.shape[:-2]
            H2, W = (lo.shape[-2], lo.shape[-1])
            x = jnp.stack([r_e, r_o], axis=-2).reshape(B + (2 * H2, W))
            return x

        def batchnorm_relu(x, gamma, beta, eps=1e-05):
            mean = jnp.mean(x, axis=(0, 2, 3), keepdims=True)
            var = jnp.var(x, axis=(0, 2, 3), keepdims=True)
            xn = (x - mean) * lax.rsqrt(var + eps)
            return jax.nn.relu(xn * gamma[None, :, None, None] + beta[None, :, None, None])
        key = jax.random.key(seed)
        ks = jax.random.split(key, 4)
        return {'x': jax.random.normal(ks[0], (16, 128, 32, 32), dtype=jnp.float32), 'conv_w': jax.random.normal(ks[1], (128, 128), dtype=jnp.float32) * 0.05, 'bn_gamma': jnp.ones((128,), jnp.float32), 'bn_beta': jnp.zeros((128,), jnp.float32), 'convW_w': jax.random.normal(ks[2], (128, 256, 3, 3), dtype=jnp.float32) * 0.02, 'convW_b': jnp.zeros((128,), jnp.float32), 'bnW_gamma': jnp.ones((128,), jnp.float32), 'bnW_beta': jnp.zeros((128,), jnp.float32)}
    _L0_conv_all = _L0_conv_setup()
    _L0_conv_in = {k: v for k, v in _L0_conv_all.items() if k in ('conv_w', 'bn_gamma', 'bn_beta', 'convW_w', 'convW_b', 'bnW_gamma', 'bnW_beta')}
    del _L0_conv_all

    def _L1_conv_setup():
        import jax, jax.numpy as jnp
        import numpy as np
        KSIZE = 3

        def median_blur(x, k):
            pad = (k - 1) // 2
            xp = jnp.pad(x, ((0, 0), (0, 0), (pad, pad), (pad, pad)))
            B, C, H, W = x.shape
            patches = jnp.stack([xp[:, :, i:i + H, j:j + W] for i in range(k) for j in range(k)], axis=-1)
            return jnp.median(patches, axis=-1)
        key = jax.random.key(seed)
        k1, k2, k3 = jax.random.split(key, 3)
        C = 128
        x = jax.random.normal(k1, (16, C, 32, 32), dtype=jnp.float32)
        W = jax.random.normal(k2, (C, C), dtype=jnp.float32) / jnp.sqrt(jnp.float32(C))
        b = jax.random.normal(k3, (C,), dtype=jnp.float32) * 0.01
        return {'x': x, 'W': W, 'b': b}
    _L1_conv_all = _L1_conv_setup()
    _L1_conv_in = {k: v for k, v in _L1_conv_all.items() if k in ('W', 'b')}
    del _L1_conv_all
    return {'x': x, 'L0_conv_conv_w': _L0_conv_in['conv_w'], 'L0_conv_bn_gamma': _L0_conv_in['bn_gamma'], 'L0_conv_bn_beta': _L0_conv_in['bn_beta'], 'L0_conv_convW_w': _L0_conv_in['convW_w'], 'L0_conv_convW_b': _L0_conv_in['convW_b'], 'L0_conv_bnW_gamma': _L0_conv_in['bnW_gamma'], 'L0_conv_bnW_beta': _L0_conv_in['bnW_beta'], 'L1_conv_W': _L1_conv_in['W'], 'L1_conv_b': _L1_conv_in['b']}

def reference(x, L0_conv_conv_w, L0_conv_bn_gamma, L0_conv_bn_beta, L0_conv_convW_w, L0_conv_convW_b, L0_conv_bnW_gamma, L0_conv_bnW_beta, L1_conv_W, L1_conv_b):
    import jax
    import jax.numpy as jnp

    def _L0_conv_ref(x, conv_w, bn_gamma, bn_beta, convW_w, convW_b, bnW_gamma, bnW_beta):
        import jax, jax.numpy as jnp
        from jax import lax
        import numpy as np
        S = 0.7071067811865476

        def dwt2(x):
            lo = (x[..., 0::2, :] + x[..., 1::2, :]) * S
            hi = (x[..., 0::2, :] - x[..., 1::2, :]) * S
            cA = (lo[..., 0::2] + lo[..., 1::2]) * S
            cV = (lo[..., 0::2] - lo[..., 1::2]) * S
            cH = (hi[..., 0::2] + hi[..., 1::2]) * S
            cD = (hi[..., 0::2] - hi[..., 1::2]) * S
            return (cA, cH, cV, cD)

        def _interleave(e, o, axis):
            s = jnp.stack([e, o], axis=axis)
            shp = list(e.shape)
            shp[axis] = shp[axis] * 2 if axis >= 0 else shp[axis] * 2
            out_shape = list(e.shape)
            out_shape[axis % e.ndim] *= 2
            return s.reshape(out_shape)

        def idwt2(cA, cH, cV, cD):
            lo_e = (cA + cV) * S
            lo_o = (cA - cV) * S
            lo = jnp.stack([lo_e, lo_o], axis=-1).reshape(cA.shape[:-1] + (cA.shape[-1] * 2,))
            hi_e = (cH + cD) * S
            hi_o = (cH - cD) * S
            hi = jnp.stack([hi_e, hi_o], axis=-1).reshape(cH.shape[:-1] + (cH.shape[-1] * 2,))
            r_e = (lo + hi) * S
            r_o = (lo - hi) * S
            B = lo.shape[:-2]
            H2, W = (lo.shape[-2], lo.shape[-1])
            x = jnp.stack([r_e, r_o], axis=-2).reshape(B + (2 * H2, W))
            return x

        def batchnorm_relu(x, gamma, beta, eps=1e-05):
            mean = jnp.mean(x, axis=(0, 2, 3), keepdims=True)
            var = jnp.var(x, axis=(0, 2, 3), keepdims=True)
            xn = (x - mean) * lax.rsqrt(var + eps)
            return jax.nn.relu(xn * gamma[None, :, None, None] + beta[None, :, None, None])
        cA, cH, cV, cD = dwt2(x)
        proc = lambda c: batchnorm_relu(jnp.einsum('bchw,oc->bohw', c, conv_w), bn_gamma, bn_beta)
        rimg0 = idwt2(proc(cA), proc(cH), proc(cV), proc(cD))
        a1, h1, v1, d1 = dwt2(x)
        a2, h2, v2, d2 = dwt2(a1)
        a3, h3, v3, d3 = dwt2(a2)
        r3 = idwt2(a3, h3, v3, d3)
        r2 = idwt2(r3, h2, v2, d2)
        rimg1 = idwt2(r2, h1, v1, d1)
        rimg = jnp.concatenate([rimg0, rimg1], axis=1)
        y = lax.conv_general_dilated(rimg, convW_w, window_strides=(1, 1), padding='SAME', dimension_numbers=('NCHW', 'OIHW', 'NCHW'))
        y = y + convW_b[None, :, None, None]
        return batchnorm_relu(y, bnW_gamma, bnW_beta)

    def _L1_conv_ref(x, W, b):
        import jax, jax.numpy as jnp
        import numpy as np
        KSIZE = 3

        def median_blur(x, k):
            pad = (k - 1) // 2
            xp = jnp.pad(x, ((0, 0), (0, 0), (pad, pad), (pad, pad)))
            B, C, H, W = x.shape
            patches = jnp.stack([xp[:, :, i:i + H, j:j + W] for i in range(k) for j in range(k)], axis=-1)
            return jnp.median(patches, axis=-1)
        x_denoised = median_blur(x, KSIZE)
        y = jnp.einsum('bchw,oc->bohw', x_denoised, W) + b[None, :, None, None]
        return x + y

    def _gn(v, G=32, eps=1e-05):
        B_, C_, H_, W_ = v.shape
        g = v.reshape(B_, G, C_ // G, H_, W_)
        m = jnp.mean(g, axis=(2, 3, 4), keepdims=True)
        s = jnp.var(g, axis=(2, 3, 4), keepdims=True)
        return ((g - m) / jnp.sqrt(s + eps)).reshape(v.shape)

    def _ln_c(v, eps=1e-06):
        m = jnp.mean(v, axis=1, keepdims=True)
        s = jnp.var(v, axis=1, keepdims=True)
        return (v - m) / jnp.sqrt(s + eps)

    def _ln_t(v, eps=1e-05):
        m = jnp.mean(v, axis=-1, keepdims=True)
        s = jnp.var(v, axis=-1, keepdims=True)
        return (v - m) / jnp.sqrt(s + eps)

    def _to_tokens(v):
        B_, C_, H_, W_ = v.shape
        return v.reshape(B_, C_, H_ * W_).transpose(0, 2, 1)

    def _from_tokens(t, like):
        B_, C_, H_, W_ = like.shape
        return t.transpose(0, 2, 1).reshape(B_, C_, H_, W_)
    x = _L0_conv_ref(x, L0_conv_conv_w, L0_conv_bn_gamma, L0_conv_bn_beta, L0_conv_convW_w, L0_conv_convW_b, L0_conv_bnW_gamma, L0_conv_bnW_beta)
    x = _L1_conv_ref(x, L1_conv_W, L1_conv_b)
    return x

_drawn_inputs = setup_inputs


def setup_inputs(seed=0):
    import zlib

    import numpy as np

    out = dict(_drawn_inputs(seed))
    spreads = {'L0_conv_bn_gamma': (1.0, 0.2),
     'L0_conv_bn_beta': (0.0, 0.1),
     'L0_conv_convW_b': (0.0, 0.8),
     'L0_conv_bnW_gamma': (1.0, 0.2),
     'L0_conv_bnW_beta': (0.0, 0.1)}
    factors = {'L1_conv_b': 4.446}
    for name, (base, spread) in spreads.items():
        noise = np.random.default_rng([zlib.crc32(name.encode()), seed]).standard_normal(out[name].shape)
        drawn = base * np.exp(spread * noise) if base else spread * noise
        out[name] = jnp.asarray(drawn.astype(out[name].dtype))
    for name, factor in factors.items():
        out[name] = (out[name] * factor).astype(out[name].dtype)
    return out
```

```python
import concourse.bass as bass
from concourse import mybir
from contextlib import ExitStack


def wavelet_conv_median_kernel(nc, x, w1_t, gamma1, beta1, w3_t, bias3, gamma3, beta3, gamma3_row, w2_t, bias2, out):
    fp32 = mybir.dt.float32
    fp32r = mybir.dt.float32r
    ALU = mybir.AluOpType
    ACT = mybir.ActivationFunctionType

    IMAGES, CH, H, W = x.shape
    PIX = H * W
    HALF = PIX // 2
    BANDS = 4
    BAND = PIX // BANDS
    BANK = 512
    BH, BW = H // 2, W // 2
    TAPS = 9
    PITCH = W + 1
    SPLIT = (H + 2) * PITCH + 1
    COLS = H * PITCH + 1
    ROWS = H + 1
    EPS = 1e-5
    LOW = -1.0e30
    XQ = 4
    PAIRS = IMAGES // 2

    x_img = x.rearrange("n c h w -> c n (h w)")
    out_img = out.rearrange("n c h w -> c n (h w)")

    ctx = ExitStack()
    with ctx:
        def sb(name, shape, dt=fp32):
            return ctx.enter_context(nc.sbuf_tensor(name, shape, dt))

        def sem(name):
            return ctx.enter_context(nc.semaphore(name))

        def at(ap, off, dims):
            return bass.AP(ap.tensor, ap.offset + off, [list(ap.ap[0])] + [list(d) for d in dims])

        y = sb("y", [CH, (IMAGES * ROWS + 1) * W])
        z = sb("z", [CH, IMAGES, PIX])
        x_hi = [sb(f"x_hi{k}", [CH, SPLIT], fp32r) for k in range(2)]
        x_lo = [sb(f"x_lo{k}", [CH, SPLIT], fp32r) for k in range(2)]
        r_hi = [sb(f"r_hi{k}", [CH, SPLIT], fp32r) for k in range(2)]
        r_lo = [sb(f"r_lo{k}", [CH, SPLIT], fp32r) for k in range(2)]
        w3_hi = sb("w3_hi", [CH, 2 * TAPS * CH], fp32r)
        w3_lo = sb("w3_lo", [CH, 2 * TAPS * CH], fp32r)
        w1 = sb("w1", [CH, CH])
        w2 = sb("w2", [CH, CH])
        scratch = sb("scratch", [CH, 2 * PIX + 3 * COLS])
        tmp1 = scratch[:, 0:PIX]
        tmp2 = scratch[:, PIX:2 * PIX]
        col_lo, col_mid, col_hi = (scratch[:, 2 * PIX + k * COLS:2 * PIX + (k + 1) * COLS] for k in range(3))
        w3_raw = scratch[:, 2 * PIX:2 * PIX + 2 * TAPS * CH]
        sgn_row = scratch[:, 2 * PIX + 2 * TAPS * CH:2 * PIX + 2 * TAPS * CH + CH]
        vec = sb("vec", [CH, 6])
        g1, b1, cb3, g3, b3, cb2 = (vec[:, k:k + 1] for k in range(6))
        stats1 = sb("stats1", [CH, BANDS, PAIRS, 6])
        stats3 = sb("stats3", [CH, 2 * IMAGES, 6])
        mv1 = sb("mv1", [CH, BANDS, 2])
        mv3 = sb("mv3", [CH, 2])
        bn1 = sb("bn1", [CH, 6, BANDS])
        bn3 = sb("bn3", [CH, 12])

        conv_ps = ctx.enter_context(nc.psum_tensor("conv_ps", [CH, 2, 2, BANK], fp32))
        one_ps = ctx.enter_context(nc.psum_tensor("one_ps", [CH, 2, 2, BANK], fp32))

        x_in = [sem(f"x_in{k}") for k in range(XQ)]
        vec_in = sem("vec_in")
        w1_in = sem("w1_in")
        w2_in = sem("w2_in")
        w3_in = sem("w3_in")
        pads_set = sem("pads_set")
        w1_halved = sem("w1_halved")
        bands_split = sem("bands_split")
        z_made = sem("z_made")
        z_kept = sem("z_kept")
        dve_done = sem("dve_done")
        act_passed = sem("act_passed")
        w3_signed = sem("w3_signed")
        w3_hi_set = sem("w3_hi_set")
        w3_ready = sem("w3_ready")
        var1_ready = sem("var1_ready")
        sd1_ready = sem("sd1_ready")
        bn1_ready = sem("bn1_ready")
        bands_normed = sem("bands_normed")
        r_made = sem("r_made")
        x_hi_set = sem("x_hi_set")
        r_hi_set = sem("r_hi_set")
        x_split = sem("x_split")
        r_split = sem("r_split")
        conv_done = sem("conv_done")
        y_kept = sem("y_kept")
        var3_ready = sem("var3_ready")
        sd3_ready = sem("sd3_ready")
        bn3_ready = sem("bn3_ready")
        med_normed = sem("med_normed")
        med_ready = sem("med_ready")
        mix_done = sem("mix_done")
        out_ready = sem("out_ready")
        out_sent = sem("out_sent")

        def slot(n):
            return y[:, bass.ds(n * (ROWS * W) + W, PIX)]

        def zslot(n):
            return z[:, n, :] if isinstance(n, int) else z[:, bass.ds(n, 1), :].rearrange("p a q -> p (a q)")

        def inner(t):
            return at(t[:, :], PITCH + 1, [[PITCH, H], [1, W]])

        def rows(ap):
            return ap.rearrange("p (h w) -> p h w", w=W)

        def fl(t):
            return t.bitcast(fp32)

        block = ctx.enter_context(nc.Block())

        @block.sync
        def _(sp):
            sp.dma_start(w1[:, :], w1_t).then_inc(w1_in, 16)
            for n in range(XQ):
                sp.dma_start(slot(n), x_img[:, n, :]).then_inc(x_in[n], 16)
            with sp.Fori(1, IMAGES // XQ) as g:
                for k in range(XQ):
                    sp.wait_ge(x_in[k], g * 16)
                    n = g * XQ + k
                    sp.dma_start(slot(n), x_img[:, bass.ds(n, 1), :]).then_inc(x_in[k], 16)
            with sp.Fori(0, IMAGES) as n:
                sp.wait_ge(out_ready, n + 1)
                sp.dma_start(out_img[:, bass.ds(n, 1), :], slot(n)).then_inc(out_sent, 16)
            sp.wait_ge(out_sent, 16 * IMAGES)

        @block.gpsimd
        def _(pool):
            for t in x_hi + x_lo + r_hi + r_lo:
                f = fl(t[:, :])
                nc.gpsimd.memset(f[:, 0:PITCH + 1], 0.0)
                nc.gpsimd.memset(at(f, 2 * PITCH, [[PITCH, H - 1]]), 0.0)
                nc.gpsimd.memset(f[:, (H + 1) * PITCH:SPLIT], 0.0)
            nc.gpsimd.memset(at(y[:, :], 0, [[ROWS * W, IMAGES + 1], [1, W]]), LOW).then_inc(pads_set, 1)
            for n in range(IMAGES):
                pool.wait_ge(med_normed, n + 1)
                nc.gpsimd.memset(at(zslot(n), 0, [[(H - 1) * W, 2], [W - 1, 2]]), 0.0).then_inc(med_ready, 1)

        @block.tensor
        def _(pe):
            def bands_through_w1(n, k, reuse):
                pe.wait_ge(bands_split, n + 1)
                if reuse:
                    pe.wait_ge(z_kept, n - 1)
                for b in range(2):
                    mm = nc.tensor.matmul(one_ps[:, k, b, :], w1[:, :], zslot(n)[:, b * BANK:(b + 1) * BANK], start=True, stop=True)
                mm.then_inc(z_made, 1)

            pe.wait_ge(w1_halved, 1)
            for n in range(2):
                bands_through_w1(n, n, False)
            with pe.Fori(1, PAIRS) as p:
                for k in range(2):
                    bands_through_w1(p * 2 + k, k, True)

            def conv_half(k, half, hi, lo, first, last):
                for tap in range(TAPS):
                    dy, dx = tap // 3, tap % 3
                    col = (half * TAPS + tap) * CH
                    for i, (wt, src) in enumerate(((w3_lo, hi), (w3_hi, hi), (w3_hi, lo))):
                        for b in range(2):
                            rhs = at(src[:, :], (b * (H // 2) + dy) * PITCH + dx, [[PITCH, H // 2], [1, W]])
                            mm = nc.tensor.matmul(conv_ps[:, k, b, :], wt[:, col:col + CH], rhs,
                                                  start=first and tap == 0 and i == 0,
                                                  stop=last and tap == TAPS - 1 and i == 2)
                return mm

            def conv_x(n, k):
                pe.wait_ge(x_split, n + 1)
                conv_half(k, 1, x_hi[k], x_lo[k], True, False)

            def conv_r(n, k):
                pe.wait_ge(r_split, n + 1)
                conv_half(k, 0, r_hi[k], r_lo[k], False, True).then_inc(conv_done, 1)

            pe.wait_ge(w3_ready, 1)
            pe.wait_ge(pads_set, 1)
            for n in range(2):
                conv_x(n, n)
            for n in range(2):
                conv_r(n, n)
            with pe.Fori(1, PAIRS) as p:
                for k in range(2):
                    n = p * 2 + k
                    pe.wait_ge(y_kept, n - 1)
                    conv_x(n, k)
                    conv_r(n, k)

            def mix(n, k, reuse):
                pe.wait_ge(med_ready, n + 1)
                if reuse:
                    pe.wait_ge(out_ready, n - 1)
                for b in range(2):
                    mm = nc.tensor.matmul(one_ps[:, k, b, :], w2[:, :], zslot(n)[:, b * BANK:(b + 1) * BANK], start=True, stop=True)
                mm.then_inc(mix_done, 1)

            pe.wait_ge(w2_in, 16)
            for n in range(2):
                mix(n, n, False)
            with pe.Fori(1, PAIRS) as p:
                for k in range(2):
                    mix(p * 2 + k, k, True)

        @block.scalar
        def _(act):
            for k, v in enumerate((gamma1, beta1, bias3, gamma3, beta3, bias2)):
                act.dma_start(vec[:, k:k + 1], v.rearrange("(c a) -> c a", a=1)).then_inc(vec_in, 16)
            act.dma_start(sgn_row, gamma3_row.partition_broadcast(CH)).then_inc(vec_in, 16)
            act.dma_start(w3_raw, w3_t.rearrange("c t o -> c (t o)")).then_inc(w3_in, 16)
            act.dma_start(w2[:, :], w2_t).then_inc(w2_in, 16)
            act.wait_ge(w1_in, 16)
            nc.scalar.mul(w1[:, :], w1[:, :], 0.5).then_inc(w1_halved, 1)

            def keep_z(n, k):
                act.wait_ge(z_made, n + 1)
                nc.scalar.activation(zslot(n), one_ps[:, k, :, :].rearrange("p a b -> p (a b)"), ACT.Identity).then_inc(z_kept, 1)

            with act.Fori(0, PAIRS) as p:
                for k in range(2):
                    keep_z(p * 2 + k, k)

            act.wait_ge(w3_signed, 1)
            nc.scalar.activation(w3_hi[:, :], w3_raw, ACT.Identity).then_inc(w3_hi_set, 1)

            def split_x(n, k):
                nc.scalar.activation(inner(x_hi[k]), rows(slot(n)), ACT.Identity).then_inc(x_hi_set, 1)

            def norm_bands(n):
                zb = zslot(n)
                for b in range(BANDS):
                    ins = nc.scalar.activation(zb[:, b * BAND:(b + 1) * BAND], zb[:, b * BAND:(b + 1) * BAND],
                                               ACT.Relu, bias=bn1[:, 5, b:b + 1], scale=bn1[:, 4, b:b + 1])
                ins.then_inc(bands_normed, 1)

            def split_r(n, k):
                act.wait_ge(r_made, n + 1)
                act.sem_inc(act_passed, 1)
                nc.scalar.activation(inner(r_hi[k]), rows(zslot(n)), ACT.Identity).then_inc(r_hi_set, 1)

            act.wait_ge(pads_set, 1)
            for n in range(2):
                split_x(n, n)
            act.wait_ge(var1_ready, 1)
            nc.scalar.sqrt(bn1[:, 1, :], bn1[:, 0, :]).then_inc(sd1_ready, 1)
            act.wait_ge(bn1_ready, 1)
            for n in range(2):
                norm_bands(n)
            for n in range(2):
                split_r(n, n)

            def keep_y(n, k):
                act.wait_ge(conv_done, n + 1)
                nc.scalar.activation(slot(n), conv_ps[:, k, :, :].rearrange("p a b -> p (a b)"), ACT.Identity).then_inc(y_kept, 1)

            with act.Fori(0, PAIRS - 1) as p:
                for k in range(2):
                    n = p * 2 + k
                    norm_bands(n + 2)
                    keep_y(n, k)
                    split_x(n + 2, k)
                    split_r(n + 2, k)
            for k in range(2):
                keep_y(IMAGES - 2 + k, k)

            act.wait_ge(var3_ready, 1)
            nc.scalar.sqrt(bn3[:, 1:2], bn3[:, 0:1]).then_inc(sd3_ready, 1)
            act.wait_ge(bn3_ready, 1)
            with act.Fori(0, IMAGES) as n:
                nc.scalar.activation(zslot(n), zslot(n), ACT.Relu, bias=bn3[:, 7:8], scale=bn3[:, 5:6]).then_inc(med_normed, 1)

        @block.vector
        def _(dve):
            count = [0]

            def after(base, back=0):
                dve.wait_ge(dve_done, base + (count[0] - back))

            def step(ins):
                count[0] += 1
                ins.then_inc(dve_done, 1)

            V = nc.vector

            def analyse(n, tmp, base, first):
                xs = slot(n)
                zb = zslot(n)
                even = at(xs, 0, [[2 * W, BH], [1, W]])
                odd = at(xs, W, [[2 * W, BH], [1, W]])
                step(V.tensor_tensor(rows(tmp[:, 0:HALF]), even, odd, ALU.add))
                step(V.tensor_tensor(rows(tmp[:, HALF:PIX]), even, odd, ALU.subtract))
                after(base)
                te = at(tmp, 0, [[HALF, 2], [2, BAND]])
                to = at(tmp, 1, [[HALF, 2], [2, BAND]])
                step(V.tensor_tensor(at(zb, 0, [[BAND, 2], [1, BAND]]), te, to, ALU.add))
                count[0] += 1
                V.tensor_tensor(at(zb, HALF, [[BAND, 2], [1, BAND]]), te, to, ALU.subtract).then_inc(bands_split, 1)
                count[0] -= 1

            def z_stats(p):
                dve.wait_ge(z_kept, 2 * p + 2)
                zz = at(z[:, 0, :], 0, [[1, 1]])
                for b in range(BANDS):
                    src = at(z[:, bass.ds(2 * p, 2), :].rearrange("c a q -> c (a q)"), b * BAND, [[PIX, 2], [1, BAND]])
                    step(V.bn_stats(stats1[:, b, bass.ds(p, 1), :].rearrange("c a s -> c (a s)"), src))

            for n in range(XQ):
                dve.wait_ge(x_in[n], 16)
                if n >= 1:
                    after(0)
                analyse(n, (tmp1, tmp2)[n % 2], 0, n == 0)
            start = count[0]
            with dve.Fori(1, IMAGES // XQ) as g:
                count[0] = 0
                for k in range(XQ):
                    dve.wait_ge(x_in[k], g * 16 + 16)
                    analyse(g * XQ + k, (tmp1, tmp2)[k % 2], (g - 1) * 20 + start, False)
                for j in range(2):
                    z_stats(g * 2 - 2 + j)
                assert count[0] == 20
            total = [start + 20 * (IMAGES // XQ - 1)]
            count[0] = total[0]
            def chain(*args, op):
                step(op(*args))
                after(0)

            dve.wait_ge(vec_in, 16 * 7)
            chain(bn3[:, 2:3], g3, 0.0, None, ALU.is_lt, op=V.tensor_scalar)
            chain(bn3[:, 2:3], bn3[:, 2:3], -2.0, 1.0, ALU.mult, ALU.add, op=V.tensor_scalar)
            chain(sgn_row, sgn_row, 0.0, None, ALU.is_lt, op=V.tensor_scalar)
            chain(sgn_row, sgn_row, -2.0, 1.0, ALU.mult, ALU.add, op=V.tensor_scalar)
            dve.wait_ge(w3_in, 16)
            V.tensor_tensor(at(w3_raw, 0, [[CH, 2 * TAPS], [1, CH]]), at(w3_raw, 0, [[CH, 2 * TAPS], [1, CH]]),
                            at(sgn_row, 0, [[0, 2 * TAPS], [1, CH]]), ALU.mult).then_inc(w3_signed, 1)
            dve.wait_ge(w3_hi_set, 1)
            V.tensor_tensor(w3_lo[:, :], w3_raw, fl(w3_hi[:, :]), ALU.subtract).then_inc(w3_ready, 1)
            dve.wait_ge(w3_ready, 1)

            for j in range(2):
                z_stats(PAIRS - 2 + j)
            after(0)

            for b in range(BANDS):
                step(V.bn_aggr(mv1[:, b, :], stats1[:, b, :, :].rearrange("c a s -> c (a s)")))
            after(0)
            V.tensor_scalar(bn1[:, 0, :], mv1[:, :, 1], EPS, None, ALU.add).then_inc(var1_ready, 1)

            def newton(out_r, t, v, s):
                chain(out_r, s, op=V.reciprocal)
                chain(t, out_r, out_r, ALU.mult, op=V.tensor_tensor)
                chain(t, t, v, ALU.mult, op=V.tensor_tensor)
                chain(t, t, -0.5, 1.5, ALU.mult, ALU.add, op=V.tensor_scalar)
                chain(out_r, out_r, t, ALU.mult, op=V.tensor_tensor)

            dve.wait_ge(var1_ready, 1)
            dve.wait_ge(sd1_ready, 1)
            newton(bn1[:, 2, :], bn1[:, 3, :], bn1[:, 0, :], bn1[:, 1, :])
            chain(bn1[:, 4, :], bn1[:, 2, :], g1, 0.5, ALU.mult, ALU.mult, op=V.tensor_scalar)
            chain(bn1[:, 3, :], mv1[:, :, 0], bn1[:, 4, :], ALU.mult, op=V.tensor_tensor)
            chain(bn1[:, 2, 0:1], b1, 0.5, None, ALU.mult, op=V.tensor_scalar)
            V.tensor_scalar(bn1[:, 5, :], bn1[:, 3, :], -1.0, bn1[:, 2, 0:1], ALU.mult, ALU.add).then_inc(bn1_ready, 1)

            def synthesise(n, base):
                zb = zslot(n)
                a_h = at(zb, 0, [[BAND, 2], [1, BAND]])
                v_d = at(zb, HALF, [[BAND, 2], [1, BAND]])
                dve.wait_ge(bands_normed, n + 1)
                step(V.tensor_tensor(at(tmp1, 0, [[HALF, 2], [2, BAND]]), a_h, v_d, ALU.add))
                step(V.tensor_tensor(at(tmp1, 1, [[HALF, 2], [2, BAND]]), a_h, v_d, ALU.subtract))
                after(base)
                low, high = rows(tmp1[:, 0:HALF]), rows(tmp1[:, HALF:PIX])
                step(V.tensor_tensor(at(zb, 0, [[2 * W, BH], [1, W]]), low, high, ALU.add))
                V.tensor_tensor(at(zb, W, [[2 * W, BH], [1, W]]), low, high, ALU.subtract).then_inc(r_made, 1)

            def prepare(n, k, base):
                synthesise(n, base)
                dve.wait_ge(x_hi_set, n + 1)
                V.tensor_tensor(inner(x_lo[k]), rows(slot(n)), fl(inner(x_hi[k])), ALU.subtract).then_inc(x_split, 1)
                dve.wait_ge(r_hi_set, n + 1)
                V.tensor_tensor(inner(r_lo[k]), rows(zslot(n)), fl(inner(r_hi[k])), ALU.subtract).then_inc(r_split, 1)

            def median(n, base):
                top = y[:, bass.ds(n * (ROWS * W), (ROWS + 1) * W)]
                dve.wait_ge(y_kept, n + 1)
                for b in range(2):
                    step(V.bn_stats(stats3[:, bass.ds(2 * n + b, 1), :].rearrange("c a s -> c (a s)"),
                                    slot(n)[:, b * BANK:(b + 1) * BANK]))
                even = at(top, W, [[2 * W, BH], [1, W]])
                odd = at(top, 2 * W, [[2 * W, BH], [1, W]])
                step(V.tensor_tensor(rows(tmp1[:, 0:HALF]), even, odd, ALU.min))
                step(V.tensor_tensor(rows(tmp1[:, HALF:PIX]), even, odd, ALU.max))
                third = at(top, 0, [[2 * W, BH], [3 * W, 2], [1, W]])
                mn = at(tmp1, 0, [[W, BH], [0, 2], [1, W]])
                mx = at(tmp1, HALF, [[W, BH], [0, 2], [1, W]])

                def cols(t):
                    return at(t, 1, [[2 * PITCH, BH], [PITCH, 2], [1, W]])

                def body(t):
                    return at(t, 1, [[PITCH, H], [1, W]])

                mid = at(tmp2, 0, [[2 * W, BH], [W, 2], [1, W]])
                after(base, 1)
                step(V.tensor_tensor(mid, mn, third, ALU.max))
                step(V.tensor_tensor(cols(col_lo), mn, third, ALU.min))
                after(base, 2)
                step(V.tensor_tensor(cols(col_hi), mx, third, ALU.max))
                after(base, 2)
                step(V.tensor_tensor(cols(col_mid), mid, mx, ALU.min))
                def pair(t, k):
                    return at(t, 1 + k, [[PITCH, H], [2, BW]])

                def outer(t):
                    return at(t, 0, [[PITCH, H], [2, BW], [3, 2]])

                def both(off):
                    return at(tmp1, off, [[BW, H], [1, BW], [0, 2]])

                def dense(t):
                    return at(t, 0, [[W, H], [2, BW], [1, 2]])

                def padded(t):
                    return at(t, 1, [[PITCH, H], [2, BW], [1, 2]])

                p1 = at(tmp1, 0, [[BW, H], [1, BW]])
                p2 = at(tmp1, HALF, [[BW, H], [1, BW]])
                after(base, 1)
                step(V.tensor_tensor(p1, pair(col_lo, 0), pair(col_lo, 1), ALU.max))
                after(base, 1)
                step(V.tensor_tensor(p2, pair(col_hi, 0), pair(col_hi, 1), ALU.min))
                after(base, 1)
                step(V.tensor_tensor(dense(tmp2), both(0), outer(col_lo), ALU.max))
                after(base)
                step(V.tensor_tensor(padded(col_lo), both(HALF), outer(col_hi), ALU.min))
                after(base, 1)
                step(V.tensor_tensor(p1, pair(col_mid, 0), pair(col_mid, 1), ALU.min))
                after(base, 1)
                step(V.tensor_tensor(p2, pair(col_mid, 0), pair(col_mid, 1), ALU.max))
                after(base)
                step(V.tensor_tensor(padded(col_hi), both(HALF), outer(col_mid), ALU.min))
                after(base)
                step(V.tensor_tensor(padded(col_hi), both(0), padded(col_hi), ALU.max))
                step(V.tensor_tensor(body(col_mid), rows(tmp2), body(col_lo), ALU.min))
                after(base)
                step(V.tensor_tensor(rows(tmp2), rows(tmp2), body(col_lo), ALU.max))
                after(base)
                step(V.tensor_tensor(rows(tmp2), rows(tmp2), body(col_hi), ALU.min))
                after(base)
                step(V.tensor_tensor(rows(zslot(n)), body(col_mid), rows(tmp2), ALU.max))

            for n in range(2):
                prepare(n, n, 0)
                after(0)
            for t in (col_lo, col_mid, col_hi):
                step(V.memset(at(t, 0, [[PITCH, H + 1]]), LOW))
            dve.wait_ge(pads_set, 1)
            start3 = count[0]
            count[0] = 0
            per_pair = 2 * (3 + 20)
            with dve.Fori(0, PAIRS - 1) as p:
                for k in range(2):
                    n = p * 2 + k
                    after(p * per_pair + start3)
                    prepare(n + 2, k, p * per_pair + start3)
                    after(p * per_pair + start3)
                    median(n, p * per_pair + start3)
            assert count[0] == per_pair, count[0]
            count[0] = start3 + per_pair * (PAIRS - 1)
            for n in range(IMAGES - 2, IMAGES):
                median(n, 0)
                after(0)

            chain(mv3[:, :], stats3[:, :, :].rearrange("c a s -> c (a s)"), op=V.bn_aggr)
            V.tensor_scalar(bn3[:, 0:1], mv3[:, 1:2], EPS, None, ALU.add).then_inc(var3_ready, 1)
            dve.wait_ge(var3_ready, 1)
            sgn = bn3[:, 2:3]
            chain(bn3[:, 8:9], g3, sgn, None, ALU.mult, op=V.tensor_scalar)
            chain(bn3[:, 9:10], cb3, sgn, None, ALU.mult, op=V.tensor_scalar)
            chain(bn3[:, 6:7], mv3[:, 0:1], bn3[:, 9:10], ALU.add, op=V.tensor_tensor)
            dve.wait_ge(sd3_ready, 1)
            newton(bn3[:, 3:4], bn3[:, 4:5], bn3[:, 0:1], bn3[:, 1:2])
            chain(bn3[:, 5:6], bn3[:, 3:4], bn3[:, 8:9], ALU.mult, op=V.tensor_tensor)
            chain(bn3[:, 6:7], bn3[:, 9:10], bn3[:, 6:7], ALU.subtract, op=V.tensor_tensor)
            chain(bn3[:, 6:7], bn3[:, 6:7], bn3[:, 5:6], ALU.mult, op=V.tensor_tensor)
            chain(bn3[:, 7:8], bn3[:, 6:7], b3, ALU.add, op=V.tensor_tensor)
            step(V.tensor_tensor(bn3[:, 10:11], bn3[:, 7:8], cb2, ALU.add))
            dve.wait_ge(dve_done, count[0])
            V.tensor_copy(bn3[:, 11:12], bn3[:, 10:11]).then_inc(bn3_ready, 1)
            start4 = count[0]
            with dve.Fori(0, IMAGES) as n:
                V.tensor_scalar(slot(n), slot(n), bn3[:, 5:6], bn3[:, 10:11], ALU.mult, ALU.add).then_inc(dve_done, 1)
                dve.wait_ge(dve_done, n + (start4 + 1))
                dve.wait_ge(mix_done, n + 1)
                V.scalar_tensor_tensor(slot(n), slot(n), cb2, at(one_ps[:, 0, 0, :], (n % 2) * (2 * BANK), [[1, PIX]]),
                                       ALU.max, ALU.add).then_inc(out_ready, 1)


def kernel(**inputs):
    import numpy as np
    import concourse.bacc as bacc
    from concourse.bass_utils import run_bass_kernel_spmd

    nc = bacc.Bacc("TRN2", target_bir_lowering=False, num_devices=1)
    w3 = np.asarray(inputs["L0_conv_convW_w"])
    o, i = w3.shape[:2]
    half = i // 2
    w3_t = w3.reshape(o, 2, half, 9).transpose(2, 1, 3, 0).reshape(half, 18, o)
    arrays = {
        "x": inputs["x"],
        "w1_t": np.asarray(inputs["L0_conv_conv_w"]).T,
        "gamma1": inputs["L0_conv_bn_gamma"],
        "beta1": inputs["L0_conv_bn_beta"],
        "w3_t": w3_t,
        "bias3": inputs["L0_conv_convW_b"],
        "gamma3": inputs["L0_conv_bnW_gamma"],
        "beta3": inputs["L0_conv_bnW_beta"],
        "gamma3_row": np.asarray(inputs["L0_conv_bnW_gamma"]).reshape(1, o),
        "w2_t": np.asarray(inputs["L1_conv_W"]).T,
        "bias2": inputs["L1_conv_b"],
    }
    arrays = {k: np.ascontiguousarray(v) for k, v in arrays.items()}
    aps = [nc.dram_tensor(k, v.shape, mybir.dt.from_np(v.dtype), kind="ExternalInput").ap() for k, v in arrays.items()]
    shape = arrays["x"].shape
    out = nc.dram_tensor("out", shape, mybir.dt.float32, kind="ExternalOutput").ap()
    wavelet_conv_median_kernel(nc, *aps, out)
    r = run_bass_kernel_spmd(nc, [arrays], core_ids=[0])
    return r.results[0]["out"]
```

```python
import concourse.bass as bass
from concourse import mybir
from contextlib import ExitStack


def wavelet_conv_median_kernel(nc, x, w1_t, gamma1, beta1, w3_t, bias3, gamma3, beta3, w2_t, bias2, out):
    fp32 = mybir.dt.float32
    fp32r = mybir.dt.float32r
    ALU = mybir.AluOpType
    ACT = mybir.ActivationFunctionType

    IMAGES, CH, H, W = x.shape
    PIX = H * W
    HALF = PIX // 2
    BANDS = 4
    BAND = PIX // BANDS
    BANK = 512
    BH, BW = H // 2, W // 2
    TAPS = 9
    PITCH = W + 1
    SPLIT = (H + 2) * PITCH + 1
    COLS = H * PITCH + 1
    ROWS = H + 1
    EPS = 1e-5
    LOW = -1.0e30
    XQ = 4
    PAIRS = IMAGES // 2
    LEAD = 4
    ACT_SHARE = 3

    x_img = x.rearrange("n c h w -> c n (h w)")
    out_img = out.rearrange("n c h w -> c n (h w)")

    ctx = ExitStack()
    with ctx:
        def sb(name, shape, dt=fp32):
            return ctx.enter_context(nc.sbuf_tensor(name, shape, dt))

        def sem(name):
            return ctx.enter_context(nc.semaphore(name))

        def at(ap, off, dims):
            return bass.AP(ap.tensor, ap.offset + off, [list(ap.ap[0])] + [list(d) for d in dims])

        y = sb("y", [CH, (IMAGES * ROWS + 1) * W])
        z = sb("z", [CH, IMAGES, PIX])
        x_hi = [sb(f"x_hi{k}", [CH, SPLIT], fp32r) for k in range(2)]
        x_lo = [sb(f"x_lo{k}", [CH, SPLIT], fp32r) for k in range(2)]
        r_hi = [sb(f"r_hi{k}", [CH, SPLIT], fp32r) for k in range(2)]
        r_lo = [sb(f"r_lo{k}", [CH, SPLIT], fp32r) for k in range(2)]
        w3_hi = sb("w3_hi", [CH, 2 * TAPS * CH], fp32r)
        w3_lo = sb("w3_lo", [CH, 2 * TAPS * CH], fp32r)
        w1 = sb("w1", [CH, CH])
        w2 = sb("w2", [CH, CH])
        sorted_cols = sb("sorted_cols", [CH, 3 * COLS])
        col_lo, col_mid, col_hi = (sorted_cols[:, k * COLS:(k + 1) * COLS] for k in range(3))
        row_pairs = [sorted_cols[:, k * PIX:(k + 1) * PIX] for k in range(2)]
        odd_rows = [sorted_cols[:, 2 * PIX + k * HALF:2 * PIX + (k + 1) * HALF] for k in range(2)]
        W3_SLOTS = -(-2 * TAPS * CH // PIX)
        w3_raw = at(z[:, IMAGES - W3_SLOTS, :], 0, [[1, 2 * TAPS * CH]])
        syn = sb("syn", [CH, PIX])
        vec = sb("vec", [CH, 6])
        g1, b1, cb3, g3, b3, cb2 = (vec[:, k:k + 1] for k in range(6))
        stats1 = sb("stats1", [CH, BANDS, PAIRS, 6])
        mv1 = sb("mv1", [CH, BANDS, 2])
        bn1 = sb("bn1", [CH, 6, BANDS])
        y_sum = sb("y_sum", [CH, IMAGES + 1])
        y_sq = sb("y_sq", [CH, IMAGES + 1])
        neg_shift = sb("neg_shift", [CH, 1])
        sgn = sb("sgn", [CH, 1])
        bn3 = sb("bn3", [CH, 12])

        conv_ps = ctx.enter_context(nc.psum_tensor("conv_ps", [CH, 2, PIX], fp32))
        one_ps = ctx.enter_context(nc.psum_tensor("one_ps", [CH, 2, PIX], fp32))
        tmp1, tmp2 = one_ps[:, 0, :], one_ps[:, 1, :]

        x_in = [sem(f"x_in{k}") for k in range(XQ)]
        vec_in = sem("vec_in")
        w1_in = sem("w1_in")
        w2_in = sem("w2_in")
        w3_in = sem("w3_in")
        pads_set = sem("pads_set")
        w1_halved = sem("w1_halved")
        z_made = sem("z_made")
        odd_kept = sem("odd_kept")
        rows_split = sem("rows_split")
        bands_made = sem("bands_made")
        dve_done = sem("dve_done")
        pool_passed = sem("pool_passed")
        act_passed = sem("act_passed")
        syn_half = sem("syn_half")
        w3_hi_set = sem("w3_hi_set")
        w3_ready = sem("w3_ready")
        sgn_ready = sem("sgn_ready")
        var1_ready = sem("var1_ready")
        sd1_ready = sem("sd1_ready")
        bn1_ready = sem("bn1_ready")
        bands_normed = sem("bands_normed")
        r_made = sem("r_made")
        x_hi_set = sem("x_hi_set")
        r_hi_set = sem("r_hi_set")
        x_split = sem("x_split")
        r_split = sem("r_split")
        conv_done = sem("conv_done")
        y_kept = sem("y_kept")
        shift_set = sem("shift_set")
        squares_summed = sem("squares_summed")
        med_made = sem("med_made")
        var3_ready = sem("var3_ready")
        sd3_ready = sem("sd3_ready")
        bn3_ready = sem("bn3_ready")
        med_normed = sem("med_normed")
        x1_made = sem("x1_made")
        med_ready = sem("med_ready")
        mix_done = sem("mix_done")
        out_ready = sem("out_ready")
        out_sent = sem("out_sent")

        def slot(n):
            return y[:, bass.ds(n * (ROWS * W) + W, PIX)]

        def zslot(n):
            return z[:, n, :] if isinstance(n, int) else z[:, bass.ds(n, 1), :].rearrange("p a q -> p (a q)")

        def inner(t):
            return at(t[:, :], PITCH + 1, [[PITCH, H], [1, W]])

        def rows(ap):
            return ap.rearrange("p (h w) -> p h w", w=W)

        def fl(t):
            return t.bitcast(fp32)

        def even_rows(ap):
            return at(ap, 0, [[2 * W, BH], [1, W]])

        def other_rows(ap):
            return at(ap, W, [[2 * W, BH], [1, W]])

        block = ctx.enter_context(nc.Block())

        @block.sync
        def _(sp):
            sp.dma_start(slot(0), x_img[:, 0, :]).then_inc(x_in[0], 16)
            sp.dma_start(w1[:, :], w1_t).then_inc(w1_in, 16)
            for n in range(1, XQ):
                sp.dma_start(slot(n), x_img[:, n, :]).then_inc(x_in[n], 16)
            with sp.Fori(1, IMAGES // XQ) as g:
                for k in range(XQ):
                    sp.wait_ge(x_in[k], g * 16)
                    n = g * XQ + k
                    sp.dma_start(slot(n), x_img[:, bass.ds(n, 1), :]).then_inc(x_in[k], 16)
            with sp.Fori(0, IMAGES) as n:
                sp.wait_ge(out_ready, n + 1)
                sp.dma_start(out_img[:, bass.ds(n, 1), :], slot(n)).then_inc(out_sent, 16)
            sp.wait_ge(out_sent, 16 * IMAGES)

        @block.gpsimd
        def _(pool):
            G = nc.gpsimd

            def passed(s, value):
                pool.wait_ge(s, value)
                pool.sem_inc(pool_passed, 1)

            for t in x_hi + x_lo + r_hi + r_lo:
                f = fl(t[:, :])
                G.memset(f[:, 0:PITCH + 1], 0.0)
                G.memset(at(f, 2 * PITCH, [[PITCH, H - 1]]), 0.0)
                G.memset(f[:, (H + 1) * PITCH:SPLIT], 0.0)
            G.memset(at(y[:, :], 0, [[ROWS * W, IMAGES + 1], [1, W]]), LOW).then_inc(pads_set, 1)

            def analyse_columns(n, k):
                passed(rows_split, n + 1)
                even = at(row_pairs[k], 0, [[HALF, 2], [2, BAND]])
                odd = at(row_pairs[k], 1, [[HALF, 2], [2, BAND]])
                G.tensor_tensor(at(zslot(n), 0, [[BAND, 2], [1, BAND]]), even, odd, ALU.add)
                G.tensor_tensor(at(zslot(n), HALF, [[BAND, 2], [1, BAND]]), even, odd, ALU.subtract).then_inc(bands_made, 1)

            for n in range(4):
                analyse_columns(n, n % 2)
            pool.wait_ge(w3_ready, 2)
            with pool.Fori(2, PAIRS) as p:
                for k in range(2):
                    analyse_columns(p * 2 + k, k)

            def prepare(n, k):
                passed(bands_normed, n + 1)
                zb = zslot(n)
                a_h = at(zb, 0, [[BAND, 2], [1, BAND]])
                v_d = at(zb, HALF, [[BAND, 2], [1, BAND]])
                G.tensor_tensor(at(syn[:, :], 0, [[HALF, 2], [2, BAND]]), a_h, v_d, ALU.add)
                G.tensor_tensor(at(syn[:, :], 1, [[HALF, 2], [2, BAND]]), a_h, v_d, ALU.subtract).then_inc(syn_half, 1)
                passed(syn_half, n - 1)
                low, high = rows(syn[:, 0:HALF]), rows(syn[:, HALF:PIX])
                G.tensor_tensor(even_rows(zb), low, high, ALU.add)
                G.tensor_tensor(other_rows(zb), low, high, ALU.subtract).then_inc(r_made, 1)
                passed(x_hi_set, n + 1)
                G.tensor_tensor(inner(x_lo[k]), rows(slot(n)), fl(inner(x_hi[k])), ALU.subtract).then_inc(x_split, 1)
                passed(r_hi_set, n + 1)
                G.tensor_tensor(inner(r_lo[k]), rows(zslot(n)), fl(inner(r_hi[k])), ALU.subtract).then_inc(r_split, 1)

            pool.wait_ge(r_made, 2)
            pool.wait_ge(x_split, 2)
            pool.wait_ge(r_split, 2)
            with pool.Fori(1, PAIRS) as p:
                for k in range(2):
                    prepare(p * 2 + k, k)

            for n in range(IMAGES):
                pool.wait_ge(med_normed, n + 1)
                G.memset(at(zslot(n), 0, [[(H - 1) * W, 2], [W - 1, 2]]), 0.0).then_inc(med_ready, 1)

        @block.tensor
        def _(pe):
            def banks(ps, k, b):
                return ps[:, k, b * BANK:(b + 1) * BANK]

            def through_w1(n):
                pe.wait_ge(x_in[n % XQ], 16 * (n // XQ + 1))
                if n >= 2:
                    pe.wait_ge(rows_split, n - 1)
                for b in range(2):
                    mm = nc.tensor.matmul(banks(one_ps, n % 2, b), w1[:, :], slot(n)[:, b * BANK:(b + 1) * BANK],
                                          start=True, stop=True)
                mm.then_inc(z_made, 1)

            PARTS = ((w3_lo, 0), (w3_hi, 0), (w3_hi, 1))

            def conv_tap(k, half, parts, tap, bs):
                dy, dx = tap // 3, tap % 3
                col = (half * TAPS + tap) * CH
                for i, (wt, part) in enumerate(PARTS):
                    for b in bs:
                        rhs = at(parts[part][:, :], (b * (H // 2) + dy) * PITCH + dx, [[PITCH, H // 2], [1, W]])
                        mm = nc.tensor.matmul(banks(conv_ps, k, b), wt[:, col:col + CH], rhs,
                                              start=half == 1 and tap == 0 and i == 0,
                                              stop=half == 0 and tap == TAPS - 1 and i == 2)
                return mm

            def conv_x(k, bs=(0, 1)):
                for tap in range(TAPS):
                    conv_tap(k, 1, (x_hi[k], x_lo[k]), tap, bs)

            def conv_r(k, bs=(0, 1)):
                for tap in range(TAPS):
                    mm = conv_tap(k, 0, (r_hi[k], r_lo[k]), tap, bs)
                mm.then_inc(conv_done, 1)

            taps = [(n, tap) for n in range(2) for tap in range(TAPS)]
            pe.wait_ge(w1_halved, 1)
            for n in range(IMAGES):
                through_w1(n)
                if n == LEAD:
                    pe.wait_ge(pads_set, 1)
                    pe.wait_ge(w3_ready, 1)
                    pe.wait_ge(x_split, 2)
                if n >= LEAD:
                    k, tap = taps.pop(0)
                    conv_tap(k, 1, (x_hi[k], x_lo[k]), tap, (0, 1))
            for k, tap in taps:
                conv_tap(k, 1, (x_hi[k], x_lo[k]), tap, (0, 1))
            pe.wait_ge(w3_ready, 2)
            for k in range(2):
                pe.wait_ge(r_split, k + 1)
                conv_r(k)
            with pe.Fori(1, PAIRS - 1) as p:
                for k in range(2):
                    n = p * 2 + k
                    pe.wait_ge(squares_summed, n - 1)
                    pe.wait_ge(x_split, n + 1)
                    conv_x(k)
                    pe.wait_ge(r_split, n + 1)
                    conv_r(k)
            n = IMAGES - 2
            pe.wait_ge(squares_summed, n - 1)
            pe.wait_ge(x_split, n + 1)
            conv_x(0)
            pe.wait_ge(r_split, n + 1)
            conv_r(0)
            pe.wait_ge(squares_summed, n)
            pe.wait_ge(x_split, n + 2)
            pe.wait_ge(r_split, n + 2)
            for b in range(2):
                conv_x(1, (b,))
                conv_r(1, (b,))

            def mix(n, k):
                pe.wait_ge(med_ready, n + 1)
                for b in range(2):
                    mm = nc.tensor.matmul(banks(conv_ps, k, b), w2[:, :], zslot(n)[:, b * BANK:(b + 1) * BANK], start=True, stop=True)
                mm.then_inc(mix_done, 1)

            pe.wait_ge(w2_in, 16)
            pe.wait_ge(squares_summed, IMAGES + 1)
            for n in range(2):
                mix(n, n)
            with pe.Fori(1, PAIRS) as p:
                for k in range(2):
                    pe.wait_ge(out_ready, p * 2 + k - 1)
                    mix(p * 2 + k, k)

        @block.scalar
        def _(act):
            act.dma_start(w3_raw, w3_t.rearrange("c t o -> c (t o)")).then_inc(w3_in, 16)
            for k, v in enumerate((gamma1, beta1, bias3, gamma3, beta3, bias2)):
                act.dma_start(vec[:, k:k + 1], v.rearrange("(c a) -> c a", a=1)).then_inc(vec_in, 16)
            act.dma_start(w2[:, :], w2_t).then_inc(w2_in, 16)
            act.wait_ge(w1_in, 16)
            nc.scalar.mul(w1[:, :], w1[:, :], 0.5).then_inc(w1_halved, 1)

            def split_x(n, k):
                nc.scalar.activation(inner(x_hi[k]), rows(slot(n)), ACT.Identity).then_inc(x_hi_set, 1)

            def split_w3(half):
                c = half * TAPS * CH
                nc.scalar.activation(w3_hi[:, c:c + TAPS * CH], w3_raw[:, c:c + TAPS * CH], ACT.Identity).then_inc(w3_hi_set, 1)

            def keep_odd(n, k):
                act.wait_ge(z_made, n + 1)
                nc.scalar.activation(rows(odd_rows[k]), other_rows(one_ps[:, k, :]), ACT.Identity).then_inc(odd_kept, 1)

            keep_odd(0, 0)
            keep_odd(1, 1)
            act.wait_ge(pads_set, 1)
            for n in range(2):
                split_x(n, n)
            act.wait_ge(w3_in, 16)
            for n in range(2):
                act.wait_ge(rows_split, n + 1)
                keep_odd(n + 2, n)
                split_w3(1 - n)
            with act.Fori(2, PAIRS) as p:
                for k in range(2):
                    act.wait_ge(rows_split, p * 2 + k - 1)
                    keep_odd(p * 2 + k, k)

            def norm_bands(n):
                zb = zslot(n)
                for b in range(BANDS):
                    ins = nc.scalar.activation(zb[:, b * BAND:(b + 1) * BAND], zb[:, b * BAND:(b + 1) * BAND],
                                               ACT.Relu, bias=bn1[:, 5, b:b + 1], scale=bn1[:, 4, b:b + 1])
                ins.then_inc(bands_normed, 1)

            def split_r(n, k):
                act.wait_ge(r_made, n + 1)
                act.sem_inc(act_passed, 1)
                nc.scalar.activation(inner(r_hi[k]), rows(zslot(n)), ACT.Identity).then_inc(r_hi_set, 1)

            act.wait_ge(var1_ready, 1)
            nc.scalar.sqrt(bn1[:, 1, :], bn1[:, 0, :]).then_inc(sd1_ready, 1)
            act.wait_ge(bn1_ready, 1)
            norm_bands(0)
            split_r(0, 0)
            norm_bands(1)
            split_r(1, 1)

            def keep_y(k, count, dst, src, s):
                act.wait_ge(conv_done, count)
                nc.scalar.activation(dst, src, ACT.Identity, scale=sgn[:, :], accum_out=s).then_inc(y_kept, 1)

            def square_y(src, s):
                nc.scalar.activation(src, src, ACT.Square, bias=neg_shift[:, :], scale=sgn[:, :], accum_out=s).then_inc(squares_summed, 1)

            def image(n, k, first=False):
                norm_bands(n + 2)
                keep_y(k, n + 1, slot(n), conv_ps[:, k, :], y_sum[:, bass.ds(n, 1)])
                split_x(n + 2, k)
                if first:
                    act.wait_ge(y_kept, 1)
                    nc.scalar.mul(neg_shift[:, :], y_sum[:, 0:1], -1.0 / PIX).then_inc(shift_set, 1)
                    act.wait_ge(shift_set, 1)
                square_y(conv_ps[:, k, :], y_sq[:, bass.ds(n, 1)])
                split_r(n + 2, k)

            act.wait_ge(sgn_ready, 1)
            image(0, 0, True)
            image(1, 1)
            with act.Fori(1, PAIRS - 1) as p:
                for k in range(2):
                    image(p * 2 + k, k)
            n = IMAGES - 2
            keep_y(0, n + 1, slot(n), conv_ps[:, 0, :], y_sum[:, n:n + 1])
            square_y(conv_ps[:, 0, :], y_sq[:, n:n + 1])
            for b in range(2):
                half = slice(b * BANK, (b + 1) * BANK)
                keep_y(1, n + 2 + b, slot(n + 1)[:, half], conv_ps[:, 1, half], y_sum[:, n + 1 + b:n + 2 + b])
                square_y(conv_ps[:, 1, half], y_sq[:, n + 1 + b:n + 2 + b])

            act.wait_ge(var3_ready, 1)
            nc.scalar.sqrt(bn3[:, 1:2], bn3[:, 0:1]).then_inc(sd3_ready, 1)
            act.wait_ge(bn3_ready, 1)
            with act.Fori(0, IMAGES // 4) as g:
                for k in range(4):
                    n = g * 4 + k
                    act.wait_ge(med_made, n + 1)
                    nc.scalar.activation(zslot(n), zslot(n), ACT.Relu, bias=bn3[:, 7:8], scale=bn3[:, 5:6]).then_inc(med_normed, 1)
                    if k < ACT_SHARE:
                        nc.scalar.activation(slot(n), slot(n), ACT.Identity, bias=bn3[:, 10:11], scale=bn3[:, 5:6]).then_inc(x1_made, 1)

        @block.vector
        def _(dve):
            count = [0]

            def after(base, back=0):
                dve.wait_ge(dve_done, base + (count[0] - back))

            def step(ins):
                count[0] += 1
                ins.then_inc(dve_done, 1)

            def chain(*args, op):
                step(op(*args))
                after(0)

            V = nc.vector

            def analyse_rows(n, k):
                dve.wait_ge(odd_kept, n + 1)
                even = even_rows(one_ps[:, k, :])
                V.tensor_tensor(rows(row_pairs[k][:, 0:HALF]), even, rows(odd_rows[k]), ALU.add)
                V.tensor_tensor(rows(row_pairs[k][:, HALF:PIX]), even, rows(odd_rows[k]), ALU.subtract).then_inc(rows_split, 1)

            def band_stats(p):
                dve.wait_ge(bands_made, 2 * p + 2)
                two = z[:, bass.ds(2 * p, 2), :].rearrange("c a q -> c (a q)")
                for b in range(BANDS):
                    ins = V.bn_stats(stats1[:, b, bass.ds(p, 1), :].rearrange("c a s -> c (a s)"),
                                     at(two, b * BAND, [[PIX, 2], [1, BAND]]))
                return ins

            for n in range(2):
                analyse_rows(n, n)
            for n in range(2):
                dve.wait_ge(x_hi_set, n + 1)
                V.tensor_tensor(inner(x_lo[n]), rows(slot(n)), fl(inner(x_hi[n])), ALU.subtract).then_inc(x_split, 1)
            for n in range(2):
                dve.wait_ge(bands_made, n + 1)
                analyse_rows(n + 2, n)
                c = (1 - n) * TAPS * CH
                dve.wait_ge(w3_hi_set, n + 1)
                V.tensor_tensor(w3_lo[:, c:c + TAPS * CH], w3_raw[:, c:c + TAPS * CH], fl(w3_hi[:, c:c + TAPS * CH]),
                                ALU.subtract).then_inc(w3_ready, 1)
            band_stats(0)
            with dve.Fori(2, PAIRS) as p:
                for k in range(2):
                    n = p * 2 + k
                    dve.wait_ge(bands_made, n - 1)
                    analyse_rows(n, k)
                band_stats(p - 1)
            dve.wait_ge(vec_in, 16 * 6)
            chain(sgn[:, :], g3, 0.0, None, ALU.is_lt, op=V.tensor_scalar)
            V.tensor_scalar(sgn[:, :], sgn[:, :], -2.0, 1.0, ALU.mult, ALU.add).then_inc(sgn_ready, 1)
            step(band_stats(PAIRS - 1))
            after(0)

            for b in range(BANDS):
                step(V.bn_aggr(mv1[:, b, :], stats1[:, b, :, :].rearrange("c a s -> c (a s)")))
            after(0)
            V.tensor_scalar(bn1[:, 0, :], mv1[:, :, 1], EPS, None, ALU.add).then_inc(var1_ready, 1)

            def newton(out_r, t, v, s):
                chain(out_r, s, op=V.reciprocal)
                chain(t, out_r, out_r, ALU.mult, op=V.tensor_tensor)
                chain(t, t, v, ALU.mult, op=V.tensor_tensor)
                chain(t, t, -0.5, 1.5, ALU.mult, ALU.add, op=V.tensor_scalar)
                chain(out_r, out_r, t, ALU.mult, op=V.tensor_tensor)

            dve.wait_ge(var1_ready, 1)
            dve.wait_ge(sd1_ready, 1)
            newton(bn1[:, 2, :], bn1[:, 3, :], bn1[:, 0, :], bn1[:, 1, :])
            chain(bn1[:, 4, :], bn1[:, 2, :], g1, 0.5, ALU.mult, ALU.mult, op=V.tensor_scalar)
            chain(bn1[:, 3, :], mv1[:, :, 0], bn1[:, 4, :], ALU.mult, op=V.tensor_tensor)
            chain(bn1[:, 2, 0:1], b1, 0.5, None, ALU.mult, op=V.tensor_scalar)
            V.tensor_scalar(bn1[:, 5, :], bn1[:, 3, :], -1.0, bn1[:, 2, 0:1], ALU.mult, ALU.add).then_inc(bn1_ready, 1)

            for t in (col_lo, col_mid, col_hi):
                step(V.memset(at(t, 0, [[PITCH, H + 1]]), LOW))

            def prepare(n, k):
                zb = zslot(n)
                a_h = at(zb, 0, [[BAND, 2], [1, BAND]])
                v_d = at(zb, HALF, [[BAND, 2], [1, BAND]])
                dve.wait_ge(bands_normed, n + 1)
                step(V.tensor_tensor(at(syn[:, :], 0, [[HALF, 2], [2, BAND]]), a_h, v_d, ALU.add))
                step(V.tensor_tensor(at(syn[:, :], 1, [[HALF, 2], [2, BAND]]), a_h, v_d, ALU.subtract))
                after(0)
                low, high = rows(syn[:, 0:HALF]), rows(syn[:, HALF:PIX])
                step(V.tensor_tensor(even_rows(zb), low, high, ALU.add))
                V.tensor_tensor(other_rows(zb), low, high, ALU.subtract).then_inc(r_made, 1)
                dve.wait_ge(r_hi_set, n + 1)
                V.tensor_tensor(inner(r_lo[k]), rows(zb), fl(inner(r_hi[k])), ALU.subtract).then_inc(r_split, 1)

            for n in range(2):
                prepare(n, n)
            after(0)

            def median(n, base, kept, pair0=0, pairs=BH):
                r0, nr = 2 * pair0, 2 * pairs
                top = y[:, bass.ds(n * (ROWS * W) + r0 * W, (nr + 2) * W)]
                res = z[:, bass.ds(n, 1), :].rearrange("p a q -> p (a q)")
                dve.wait_ge(y_kept, kept)
                even = at(top, W, [[2 * W, pairs], [1, W]])
                odd = at(top, 2 * W, [[2 * W, pairs], [1, W]])
                third = at(top, 0, [[2 * W, pairs], [3 * W, 2], [1, W]])

                def sorted_rows(off):
                    return at(tmp1, off, [[W, pairs], [1, W]])

                def twice(off):
                    return at(tmp1, off, [[W, pairs], [0, 2], [1, W]])

                def cols(t):
                    return at(t, r0 * PITCH + 1, [[2 * PITCH, pairs], [PITCH, 2], [1, W]])

                step(V.tensor_tensor(sorted_rows(0), even, odd, ALU.min))
                step(V.tensor_tensor(sorted_rows(HALF), even, odd, ALU.max))
                after(base, 1)
                step(V.tensor_tensor(cols(col_mid), twice(0), third, ALU.max))
                step(V.tensor_tensor(cols(col_lo), twice(0), third, ALU.min))
                after(base, 2)
                step(V.tensor_tensor(cols(col_hi), twice(HALF), third, ALU.max))
                after(base, 2)
                step(V.tensor_tensor(cols(col_mid), twice(HALF), cols(col_mid), ALU.min))

                def pair(t, k):
                    return at(t, r0 * PITCH + 1 + k, [[PITCH, nr], [2, BW]])

                def outer(t):
                    return at(t, r0 * PITCH, [[PITCH, nr], [2, BW], [3, 2]])

                def both(off):
                    return at(tmp1, off, [[BW, nr], [1, BW], [0, 2]])

                def padded(t):
                    return at(t, r0 * PITCH + 1, [[PITCH, nr], [2, BW], [1, 2]])

                def body(t):
                    return at(t, r0 * PITCH + 1, [[PITCH, nr], [1, W]])

                p1 = at(tmp1, 0, [[BW, nr], [1, BW]])
                p2 = at(tmp1, HALF, [[BW, nr], [1, BW]])
                dense3 = at(tmp2, 0, [[W, nr], [2, BW], [1, 2]])
                dense = at(tmp2, 0, [[W, nr], [1, W]])
                after(base, 1)
                step(V.tensor_tensor(p1, pair(col_lo, 0), pair(col_lo, 1), ALU.max))
                after(base, 1)
                step(V.tensor_tensor(p2, pair(col_hi, 0), pair(col_hi, 1), ALU.min))
                after(base, 1)
                step(V.tensor_tensor(dense3, both(0), outer(col_lo), ALU.max))
                after(base)
                step(V.tensor_tensor(padded(col_lo), both(HALF), outer(col_hi), ALU.min))
                after(base, 1)
                step(V.tensor_tensor(p1, pair(col_mid, 0), pair(col_mid, 1), ALU.min))
                after(base, 1)
                step(V.tensor_tensor(p2, pair(col_mid, 0), pair(col_mid, 1), ALU.max))
                after(base)
                step(V.tensor_tensor(padded(col_hi), both(HALF), outer(col_mid), ALU.min))
                after(base)
                step(V.tensor_tensor(padded(col_hi), both(0), padded(col_hi), ALU.max))
                step(V.tensor_tensor(body(col_mid), dense, body(col_lo), ALU.min))
                after(base)
                step(V.tensor_tensor(dense, dense, body(col_lo), ALU.max))
                after(base)
                step(V.tensor_tensor(dense, dense, body(col_hi), ALU.min))
                after(base)
                return V.tensor_tensor(at(res, r0 * W, [[W, nr], [1, W]]), dense, body(col_mid), ALU.max)

            MED_STEPS = 17
            dve.wait_ge(pads_set, 1)
            start = count[0]
            with dve.Fori(0, IMAGES - 1) as n:
                count[0] = 0
                median(n, n * MED_STEPS + start, n + 1).then_inc(med_made, 1)
                assert count[0] == MED_STEPS
                dve.wait_ge(med_made, n + 1)
            count[0] = start + MED_STEPS * (IMAGES - 1)
            last = IMAGES - 1
            TOP = BH // 2 - 1
            step(median(last, 0, last + 1, 0, TOP))
            after(0)

            dve.wait_ge(squares_summed, IMAGES + 1)
            step(V.reduce_sum(bn3[:, 2:3], y_sum[:, :], axis=mybir.AxisListType.X))
            chain(bn3[:, 3:4], y_sq[:, :], mybir.AxisListType.X, op=V.reduce_sum)
            N = IMAGES * PIX
            chain(bn3[:, 2:3], bn3[:, 2:3], 1.0 / N, None, ALU.mult, op=V.tensor_scalar)
            chain(bn3[:, 4:5], bn3[:, 2:3], neg_shift[:, :], ALU.add, op=V.tensor_tensor)
            chain(bn3[:, 4:5], bn3[:, 4:5], bn3[:, 4:5], ALU.mult, op=V.tensor_tensor)
            chain(bn3[:, 3:4], bn3[:, 3:4], 1.0 / N, EPS, ALU.mult, ALU.add, op=V.tensor_scalar)
            V.tensor_tensor(bn3[:, 0:1], bn3[:, 3:4], bn3[:, 4:5], ALU.subtract).then_inc(var3_ready, 1)
            dve.wait_ge(var3_ready, 1)
            chain(bn3[:, 8:9], g3, sgn[:, :], ALU.mult, op=V.tensor_tensor)
            chain(bn3[:, 9:10], cb3, sgn[:, :], ALU.mult, op=V.tensor_tensor)
            chain(bn3[:, 6:7], bn3[:, 2:3], bn3[:, 9:10], ALU.add, op=V.tensor_tensor)
            chain(bn3[:, 6:7], bn3[:, 9:10], bn3[:, 6:7], ALU.subtract, op=V.tensor_tensor)
            dve.wait_ge(sd3_ready, 1)
            newton(bn3[:, 3:4], bn3[:, 4:5], bn3[:, 0:1], bn3[:, 1:2])
            chain(bn3[:, 5:6], bn3[:, 3:4], bn3[:, 8:9], ALU.mult, op=V.tensor_tensor)
            chain(bn3[:, 6:7], bn3[:, 6:7], bn3[:, 5:6], ALU.mult, op=V.tensor_tensor)
            chain(bn3[:, 7:8], bn3[:, 6:7], b3, ALU.add, op=V.tensor_tensor)
            V.tensor_tensor(bn3[:, 10:11], bn3[:, 7:8], cb2, ALU.add).then_inc(bn3_ready, 1)

            median(last, 0, last + 2, TOP, BH - TOP).then_inc(med_made, 1)

            dve.wait_ge(bn3_ready, 1)
            start = count[0]
            with dve.Fori(0, IMAGES // 4) as g:
                for k in range(4):
                    n = g * 4 + k
                    if k >= ACT_SHARE:
                        V.tensor_scalar(slot(n), slot(n), bn3[:, 5:6], bn3[:, 10:11], ALU.mult, ALU.add).then_inc(dve_done, 1)
                        dve.wait_ge(dve_done, g * (4 - ACT_SHARE) + (start + 1 + k - ACT_SHARE))
                    else:
                        dve.wait_ge(x1_made, g * ACT_SHARE + (k + 1))
                    dve.wait_ge(mix_done, n + 1)
                    V.scalar_tensor_tensor(slot(n), slot(n), cb2, conv_ps[:, k % 2, :], ALU.max, ALU.add).then_inc(out_ready, 1)


def kernel(**inputs):
    import numpy as np
    import concourse.bacc as bacc
    from concourse.bass_utils import run_bass_kernel_spmd

    nc = bacc.Bacc("TRN2", target_bir_lowering=False, num_devices=1)
    w3 = np.asarray(inputs["L0_conv_convW_w"])
    o, i = w3.shape[:2]
    half = i // 2
    w3_t = w3.reshape(o, 2, half, 9).transpose(2, 1, 3, 0).reshape(half, 18, o)
    arrays = {
        "x": inputs["x"],
        "w1_t": np.asarray(inputs["L0_conv_conv_w"]).T,
        "gamma1": inputs["L0_conv_bn_gamma"],
        "beta1": inputs["L0_conv_bn_beta"],
        "w3_t": w3_t,
        "bias3": inputs["L0_conv_convW_b"],
        "gamma3": inputs["L0_conv_bnW_gamma"],
        "beta3": inputs["L0_conv_bnW_beta"],
        "w2_t": np.asarray(inputs["L1_conv_W"]).T,
        "bias2": inputs["L1_conv_b"],
    }
    arrays = {k: np.ascontiguousarray(v) for k, v in arrays.items()}
    aps = [nc.dram_tensor(k, v.shape, mybir.dt.from_np(v.dtype), kind="ExternalInput").ap() for k, v in arrays.items()]
    shape = arrays["x"].shape
    out = nc.dram_tensor("out", shape, mybir.dt.float32, kind="ExternalOutput").ap()
    wavelet_conv_median_kernel(nc, *aps, out)
    r = run_bass_kernel_spmd(nc, [arrays], core_ids=[0])
    return r.results[0]["out"]
```

```python
import concourse.bass as bass
from concourse import mybir
from contextlib import ExitStack


def wavelet_conv_median_kernel(nc, x, w1_t, w3_t, w2_t, vectors, out):
    fp32 = mybir.dt.float32
    fp32r = mybir.dt.float32r
    ALU = mybir.AluOpType
    ACT = mybir.ActivationFunctionType

    IMAGES, CH, H, W = x.shape
    PIX = H * W
    HALF = PIX // 2
    BANDS = 4
    BAND = PIX // BANDS
    DIAG = BANDS - 1
    BANK = 512
    BH, BW = H // 2, W // 2
    TAPS = 9
    PITCH = W + 1
    COLS = H * PITCH + 1
    ROWS = H + 1
    EPS = 1e-5
    LOW = -1.0e30
    XQ = 4
    PAIRS = IMAGES // 2
    WARM_UP, KEEP_WARM = 8, 24
    LEAD = 5
    FILLS = (3, 2, 1, 2, 1, 2, 1, 2, 1, 2, 0)
    BN3_AT, FINISH_AT = 9, (19, 20, 22, 24, 25, 27, 28, 30, 31, 32, 34, 35)
    SPLIT_IMAGES = 4
    ACT_SHARE = 1
    PIECES = {n: [(0, H // 2, 0), (H // 2, H // 2, 1)] for n in range(IMAGES - SPLIT_IMAGES, IMAGES)}
    PIECES[IMAGES - 1] = [(0, H // 2, 0), (H // 2, H // 4, 1), (3 * H // 4, H // 4, 2)]
    WHOLE = IMAGES - SPLIT_IMAGES
    PARTS_ALL = WHOLE + sum(len(v) for v in PIECES.values())

    x_img = x.rearrange("n c h w -> c n (h w)")
    out_img = out.rearrange("n c h w -> c n (h w)")

    ctx = ExitStack()
    with ctx:
        def sb(name, shape, dt=fp32):
            return ctx.enter_context(nc.sbuf_tensor(name, shape, dt))

        def sem(name):
            return ctx.enter_context(nc.semaphore(name))

        def at(ap, off, dims):
            return bass.AP(ap.tensor, ap.offset + off, [list(ap.ap[0])] + [list(d) for d in dims])

        y = sb("y", [CH, (IMAGES * ROWS + 1) * W])
        z = sb("z", [CH, IMAGES, PIX])
        x_hi = [sb(f"x_hi{k}", [CH, COLS], fp32r) for k in range(2)]
        x_lo = [sb(f"x_lo{k}", [CH, COLS], fp32r) for k in range(2)]
        r_hi = [sb(f"r_hi{k}", [CH, COLS], fp32r) for k in range(2)]
        r_lo = [sb(f"r_lo{k}", [CH, COLS], fp32r) for k in range(2)]
        w3_hi = sb("w3_hi", [CH, 2 * TAPS * CH], fp32r)
        w3_lo = sb("w3_lo", [CH, 2 * TAPS * CH], fp32r)
        w1 = sb("w1", [CH, CH])
        w2 = sb("w2", [CH, CH])
        sorted_cols = sb("sorted_cols", [CH, 3 * COLS])
        col_lo, col_mid, col_hi = (sorted_cols[:, k * COLS:(k + 1) * COLS] for k in range(3))
        row_pairs = [sorted_cols[:, k * PIX:(k + 1) * PIX] for k in range(2)]
        odd_rows = [sorted_cols[:, 2 * PIX + k * HALF:2 * PIX + (k + 1) * HALF] for k in range(2)]
        syn = sb("syn", [CH, max(PIX, TAPS * CH)])
        W3_SLOTS = -(-TAPS * CH // PIX)
        w3_raw = [syn[:, 0:TAPS * CH], at(z[:, IMAGES - W3_SLOTS, :], 0, [[1, TAPS * CH]])]
        vec = sb("vec", [CH, 6])
        g1, b1, cb3, g3, b3, cb2 = (vec[:, k:k + 1] for k in range(6))
        stats1 = sb("stats1", [CH, DIAG, PAIRS + 1, 6])
        diag_sum = sb("diag_sum", [CH, PAIRS + 1])
        diag_sq = sb("diag_sq", [CH, PAIRS + 1])
        diag_neg_shift = sb("diag_neg_shift", [CH, 1])
        diag_total, diag_sq_total, diag_off, diag_neg_off, diag_sq_mean = (
            sb(n, [CH, 1]) for n in ("diag_total", "diag_sq_total", "diag_off", "diag_neg_off", "diag_sq_mean"))
        mv1 = sb("mv1", [CH, BANDS, 2])
        bn1 = sb("bn1", [CH, 6, BANDS])
        half_bn1 = sb("half_bn1", [CH, 2])
        y_sum = sb("y_sum", [CH, PARTS_ALL])
        y_sq = sb("y_sq", [CH, PARTS_ALL])
        neg_shift = sb("neg_shift", [CH, 1])
        sgn = sb("sgn", [CH, 1])
        zeros = sb("zeros", [CH, BANK], mybir.dt.bfloat16)
        abs_g3, neg_abs_g3, signed_b, beta_bias2 = (sb(n, [CH, 1]) for n in ("abs_g3", "neg_abs_g3", "signed_b", "beta_bias2"))
        y_total, sq_total, mean3, off3, neg_off3, sq_eps3, var3, sd3, r3, newton3, scale3, neg_scale3, shift3, shift3_bias2, mid3 = (
            sb(n, [CH, 1]) for n in ("y_total", "sq_total", "mean3", "off3", "neg_off3", "sq_eps3", "var3", "sd3", "r3",
                                     "newton3", "scale3", "neg_scale3", "shift3", "shift3_bias2", "mid3"))

        conv_ps = ctx.enter_context(nc.psum_tensor("conv_ps", [CH, 2, PIX], fp32))
        conv_banks = [conv_ps[:, b // 2, (b % 2) * BANK:(b % 2 + 1) * BANK] for b in range(4)]
        one_ps = ctx.enter_context(nc.psum_tensor("one_ps", [CH, 2, PIX], fp32))
        tmp1, tmp2 = one_ps[:, 0, :], one_ps[:, 1, :]

        x_in = [sem(f"x_in{k}") for k in range(XQ)]
        x_half_in = sem("x_half_in")
        z_half_made = sem("z_half_made")
        odd_half_kept = sem("odd_half_kept")
        rows_half_split = sem("rows_half_split")
        vec_in = sem("vec_in")
        w1_in = sem("w1_in")
        w2_in = sem("w2_in")
        w3_in = [sem(f"w3_in{k}") for k in range(2)]
        pads_set = sem("pads_set")
        w1_halved = sem("w1_halved")
        z_made = sem("z_made")
        odd_kept = sem("odd_kept")
        rows_split = sem("rows_split")
        bands_made = sem("bands_made")
        diag_summed = sem("diag_summed")
        diag_shift_set = sem("diag_shift_set")
        dve_done = sem("dve_done")
        pool_passed = sem("pool_passed")
        act_passed = sem("act_passed")
        syn_half = sem("syn_half")
        w3_hi_set = sem("w3_hi_set")
        w3_ready = sem("w3_ready")
        sgn_ready = sem("sgn_ready")
        var1_ready = sem("var1_ready")
        sd1_ready = sem("sd1_ready")
        bn1_ready = sem("bn1_ready")
        bands_normed = sem("bands_normed")
        r_made = sem("r_made")
        x_hi_set = sem("x_hi_set")
        r_hi_set = sem("r_hi_set")
        x_split = sem("x_split")
        r_split = sem("r_split")
        conv_done = sem("conv_done")
        y_kept = sem("y_kept")
        shift_set = sem("shift_set")
        squares_summed = sem("squares_summed")
        med_made = sem("med_made")
        var3_ready = sem("var3_ready")
        sd3_ready = sem("sd3_ready")
        bn3_ready = sem("bn3_ready")
        half_normed = sem("half_normed")
        half_ready = sem("half_ready")
        med_normed = sem("med_normed")
        x1_by_act = sem("x1_by_act")
        x1_by_pool = sem("x1_by_pool")
        warm = sem("warm")
        med_ready = sem("med_ready")
        mix_done = sem("mix_done")
        out_ready = sem("out_ready")
        out_sent = sem("out_sent")

        def parts_before(n):
            return min(n, WHOLE) + sum(len(PIECES[m]) for m in range(WHOLE, n))

        def piece_bank(n, bank):
            return (2 * (n % 2) + bank) % 4

        def slot(n):
            return y[:, bass.ds(n * (ROWS * W) + W, PIX)]

        def zslot(n):
            return z[:, n, :] if isinstance(n, int) else z[:, bass.ds(n, 1), :].rearrange("p a q -> p (a q)")

        def inner(t):
            return at(t[:, :], 1, [[PITCH, H], [1, W]])

        def rows(ap):
            return ap.rearrange("p (h w) -> p h w", w=W)

        def fl(t):
            return t.bitcast(fp32)

        def even_rows(ap):
            return at(ap, 0, [[2 * W, BH], [1, W]])

        def other_rows(ap):
            return at(ap, W, [[2 * W, BH], [1, W]])

        block = ctx.enter_context(nc.Block())

        @block.sync
        def _(sp):
            sp.dma_start(w1[:, :], w1_t).then_inc(w1_in, 16)
            w3_cols = w3_t.rearrange("c t o -> c (t o)")
            sp.dma_start(slot(0)[:, 0:HALF], x_img[:, 0, 0:HALF]).then_inc(x_half_in, 16)
            sp.dma_start(slot(0)[:, HALF:PIX], x_img[:, 0, HALF:PIX]).then_inc(x_in[0], 16)
            for n in range(1, XQ):
                sp.dma_start(slot(n), x_img[:, n, :]).then_inc(x_in[n], 16)
                if n == 2:
                    sp.dma_start(w3_raw[1], w3_cols[:, TAPS * CH:2 * TAPS * CH]).then_inc(w3_in[1], 16)
            sp.dma_start(w3_raw[0], w3_cols[:, 0:TAPS * CH]).then_inc(w3_in[0], 16)
            sp.dma_start(vec[:, :], vectors).then_inc(vec_in, 16)
            sp.dma_start(w2[:, :], w2_t).then_inc(w2_in, 16)
            with sp.Fori(1, IMAGES // XQ) as g:
                for k in range(XQ):
                    sp.wait_ge(x_in[k], g * 16)
                    n = g * XQ + k
                    sp.dma_start(slot(n), x_img[:, bass.ds(n, 1), :]).then_inc(x_in[k], 16)
            with sp.Fori(0, IMAGES - 1) as n:
                sp.wait_ge(out_ready, n + 1)
                sp.dma_start(out_img[:, bass.ds(n, 1), :], slot(n)).then_inc(out_sent, 16)
            for part in range(2):
                sp.wait_ge(out_ready, IMAGES + part)
                half = slice(part * HALF, (part + 1) * HALF)
                sp.dma_start(out_img[:, IMAGES - 1, half], slot(IMAGES - 1)[:, half]).then_inc(out_sent, 16)
            sp.wait_ge(out_sent, 16 * (IMAGES + 1))

        @block.gpsimd
        def _(pool):
            G = nc.gpsimd

            def passed(s, value):
                pool.wait_ge(s, value)
                pool.sem_inc(pool_passed, 1)

            for t in x_hi + x_lo + r_hi + r_lo:
                G.memset(at(fl(t[:, :]), 0, [[PITCH, H + 1]]), 0.0)
            G.memset(at(y[:, :], 0, [[ROWS * W, IMAGES + 1], [1, W]]), LOW).then_inc(pads_set, 1)

            def analyse_columns(n, k, first=0, count=BAND):
                even = at(row_pairs[k], first, [[HALF, 2], [1, count]])
                odd = at(row_pairs[k], BAND + first, [[HALF, 2], [1, count]])
                G.tensor_tensor(at(zslot(n), first, [[BAND, 2], [1, count]]), even, odd, ALU.add)
                return G.tensor_tensor(at(zslot(n), HALF + first, [[BAND, 2], [1, count]]), even, odd, ALU.subtract)

            pool.wait_ge(rows_half_split, 1)
            analyse_columns(0, 0, 0, BAND // 2)
            pool.wait_ge(rows_split, 1)
            analyse_columns(0, 0, BAND // 2, BAND // 2).then_inc(bands_made, 1)
            for n in range(1, 4):
                pool.wait_ge(rows_split, n + 1)
                analyse_columns(n, n % 2).then_inc(bands_made, 1)
            pool.wait_ge(w3_ready, 1)
            with pool.Fori(2, PAIRS) as p:
                for k in range(2):
                    passed(rows_split, p * 2 + k + 1)
                    analyse_columns(p * 2 + k, k).then_inc(bands_made, 1)

            pool.wait_ge(x_hi_set, 2)
            pool.wait_ge(x_split, 1)
            G.tensor_tensor(inner(x_lo[1]), rows(slot(1)), fl(inner(x_hi[1])), ALU.subtract).then_inc(x_split, 1)

            def prepare(n, k):
                passed(bands_normed, n + 1)
                zb = zslot(n)
                a_h = at(zb, 0, [[BAND, 2], [1, BAND]])
                v_d = at(zb, HALF, [[BAND, 2], [1, BAND]])
                G.tensor_tensor(at(syn[:, :], 0, [[HALF, 2], [2, BAND]]), a_h, v_d, ALU.add)
                G.tensor_tensor(at(syn[:, :], 1, [[HALF, 2], [2, BAND]]), a_h, v_d, ALU.subtract).then_inc(syn_half, 1)
                passed(syn_half, n - 1)
                low, high = rows(syn[:, 0:HALF]), rows(syn[:, HALF:PIX])
                G.tensor_tensor(even_rows(zb), low, high, ALU.add)
                G.tensor_tensor(other_rows(zb), low, high, ALU.subtract).then_inc(r_made, 1)
                passed(x_hi_set, n + 1)
                G.tensor_tensor(inner(x_lo[k]), rows(slot(n)), fl(inner(x_hi[k])), ALU.subtract).then_inc(x_split, 1)
                passed(r_hi_set, n + 1)
                G.tensor_tensor(inner(r_lo[k]), rows(zslot(n)), fl(inner(r_hi[k])), ALU.subtract).then_inc(r_split, 1)

            pool.wait_ge(r_made, 2)
            pool.wait_ge(x_split, 2)
            pool.wait_ge(r_split, 2)
            with pool.Fori(1, PAIRS) as p:
                for k in range(2):
                    prepare(p * 2 + k, k)

            def map_x1(n):
                G.tensor_scalar(slot(n), slot(n), scale3[:, :], shift3_bias2[:, :], ALU.mult, ALU.add).then_inc(x1_by_pool, 1)

            pool.wait_ge(bn3_ready, 1)
            for b in range(2):
                pool.wait_ge(half_normed, b + 1)
                G.memset(at(zslot(0), b * (H - 1) * W, [[W - 1, 2]]), 0.0).then_inc(half_ready, 1)
            map_x1(0)
            for n in range(1, IMAGES):
                pool.wait_ge(med_normed, n)
                G.memset(at(zslot(n), 0, [[(H - 1) * W, 2], [W - 1, 2]]), 0.0).then_inc(med_ready, 1)
                if n % 4 < 4 - ACT_SHARE:
                    map_x1(n)

        @block.tensor
        def _(pe):
            def banks(ps, k, b):
                return ps[:, k, b * BANK:(b + 1) * BANK]

            def through_w1(n):
                if n >= 2:
                    pe.wait_ge(rows_split, n - 1)
                for b in range(2):
                    if n == 0 and b == 0:
                        pe.wait_ge(x_half_in, 16)
                    else:
                        pe.wait_ge(x_in[n % XQ], 16 * (n // XQ + 1))
                    if n == 0 and b == 1:
                        mm.then_inc(z_half_made, 1)
                    mm = nc.tensor.matmul(banks(one_ps, n % 2, b), w1[:, :], slot(n)[:, b * BANK:(b + 1) * BANK],
                                          start=True, stop=True)
                mm.then_inc(z_made, 1)

            PARTS = ((w3_lo, 0), (w3_hi, 0), (w3_hi, 1))

            def both_banks(k):
                return [(0, H // 2, 2 * k), (H // 2, H // 2, 2 * k + 1)]

            TAP_ORDER = sorted(range(TAPS), key=lambda tap: tap != TAPS // 2)
            FIRST_TAP, LAST_TAP = TAP_ORDER[0], TAP_ORDER[-1]

            def conv_tap(half, parts, tap, pieces, products=range(3)):
                dy, dx = tap // 3 - 1, tap % 3 - 1
                col = (half * TAPS + tap) * CH
                for i, (wt, part) in ((i, PARTS[i]) for i in products):
                    for row, nrows, bank in pieces:
                        r0, r1 = max(row, -dy), min(row + nrows, H - dy)
                        rhs = at(parts[part][:, :], (r0 + dy) * PITCH + 1 + dx, [[PITCH, r1 - r0], [1, W]])
                        mm = nc.tensor.matmul(conv_banks[bank][:, (r0 - row) * W:(r1 - row) * W], wt[:, col:col + CH], rhs,
                                              start=half == 1 and tap == FIRST_TAP and i == 0,
                                              stop=half == 0 and tap == LAST_TAP and i == 2)
                return mm

            def conv_x(k, pieces):
                for tap in TAP_ORDER:
                    conv_tap(1, (x_hi[k], x_lo[k]), tap, pieces)

            def conv_r(k, pieces):
                for tap in TAP_ORDER:
                    mm = conv_tap(0, (r_hi[k], r_lo[k]), tap, pieces)
                mm.then_inc(conv_done, 1)

            def x_product(k, tap, product):
                conv_tap(1, (x_hi[k], x_lo[k]), tap, both_banks(k), (product,))

            early = [(0, tap, product) for tap in TAP_ORDER for product in range(3)]
            pe.wait_ge(warm, 1)
            for _ in range(WARM_UP):
                nc.tensor.matmul(conv_banks[0], zeros[:, 0:CH], zeros[:, :], start=True, stop=True)
            pe.wait_ge(w1_halved, 1)
            for n in range(IMAGES):
                through_w1(n)
                if n == LEAD:
                    pe.wait_ge(pads_set, 1)
                    pe.wait_ge(w3_ready, 1)
                    pe.wait_ge(x_split, 1)
                for _ in range(FILLS[n - LEAD] if n >= LEAD else 0):
                    x_product(*early.pop(0))
            for k_tap_product in early:
                x_product(*k_tap_product)
            pe.wait_ge(x_hi_set, 2)
            for tap in TAP_ORDER:
                conv_tap(1, (x_hi[1], x_lo[1]), tap, both_banks(1), (0, 1))
            pe.wait_ge(x_split, 2)
            for tap in TAP_ORDER:
                conv_tap(1, (x_hi[1], x_lo[1]), tap, both_banks(1), (2,))
            pe.wait_ge(w3_ready, 2)
            pe.wait_ge(r_hi_set, 1)
            for tap in TAP_ORDER:
                conv_tap(0, (r_hi[0], r_lo[0]), tap, both_banks(0), (0, 1))
            pe.wait_ge(r_split, 1)
            for tap in TAP_ORDER:
                mm = conv_tap(0, (r_hi[0], r_lo[0]), tap, both_banks(0), (2,))
            mm.then_inc(conv_done, 1)
            pe.wait_ge(r_split, 2)
            conv_r(1, both_banks(1))
            with pe.Fori(1, WHOLE // 2) as p:
                for k in range(2):
                    n = p * 2 + k
                    pe.wait_ge(squares_summed, n - 1)
                    pe.wait_ge(x_split, n + 1)
                    conv_x(k, both_banks(k))
                    pe.wait_ge(r_split, n + 1)
                    conv_r(k, both_banks(k))
            for n in range(WHOLE, IMAGES):
                pe.wait_ge(squares_summed, parts_before(n - 1))
                pe.wait_ge(x_split, n + 1)
                pe.wait_ge(r_split, n + 1)
                for row, nrows, bank in PIECES[n]:
                    if bank == 2:
                        pe.wait_ge(squares_summed, parts_before(n))
                    piece = (row, nrows, piece_bank(n, bank))
                    conv_x(n % 2, [piece])
                    conv_r(n % 2, [piece])

            def mix(n, k):
                if n > 0:
                    pe.wait_ge(med_ready, n)
                for b in range(2):
                    if n == 0:
                        pe.wait_ge(half_ready, b + 1)
                    mm = nc.tensor.matmul(banks(conv_ps, k, b), w2[:, :], zslot(n)[:, b * BANK:(b + 1) * BANK], start=True, stop=True)
                    if b == 1 or n == IMAGES - 1:
                        mm.then_inc(mix_done, 1)

            for _ in range(KEEP_WARM):
                nc.tensor.matmul(conv_banks[1], zeros[:, 0:CH], zeros[:, :], start=True, stop=True)
            pe.wait_ge(w2_in, 16)
            pe.wait_ge(squares_summed, PARTS_ALL)
            for n in range(2):
                mix(n, n)
            for n in range(2, IMAGES):
                pe.wait_ge(out_ready, n - 1)
                mix(n, n % 2)

        @block.scalar
        def _(act):
            act.wait_ge(w1_in, 16)
            nc.scalar.mul(w1[:, :], w1[:, :], 0.5).then_inc(w1_halved, 1)

            def split_x(n, k):
                nc.scalar.activation(inner(x_hi[k]), rows(slot(n)), ACT.Identity).then_inc(x_hi_set, 1)

            def split_w3(half):
                c = half * TAPS * CH
                nc.scalar.activation(w3_hi[:, c:c + TAPS * CH], w3_raw[half], ACT.Identity).then_inc(w3_hi_set, 1)

            def keep_odd(n, k):
                act.wait_ge(z_made, n + 1)
                nc.scalar.activation(rows(odd_rows[k]), other_rows(one_ps[:, k, :]), ACT.Identity).then_inc(odd_kept, 1)

            upper, lower = (at(one_ps[:, 0, :], b * BANK + W, [[2 * W, BH // 2], [1, W]]) for b in range(2))
            act.wait_ge(z_half_made, 1)
            nc.scalar.activation(rows(odd_rows[0][:, 0:HALF // 2]), upper, ACT.Identity).then_inc(odd_half_kept, 1)
            act.wait_ge(z_made, 1)
            nc.scalar.activation(rows(odd_rows[0][:, HALF // 2:HALF]), lower, ACT.Identity).then_inc(odd_kept, 1)
            act.wait_ge(pads_set, 1)
            split_x(0, 0)
            keep_odd(1, 1)
            split_x(1, 1)
            for n in range(2):
                act.wait_ge(rows_split, n + 1)
                keep_odd(n + 2, n)
                act.wait_ge(w3_in[1 - n], 16)
                split_w3(1 - n)

            def diag(value, shape):
                return at(w3_lo[:, :], value * 2 * BAND, shape)

            def diag_sums(src, shape, group, first=False):
                total, squares = (t[:, bass.ds(group, 1)] for t in (diag_sum, diag_sq))
                nc.scalar.activation(diag(0, shape), src, ACT.Identity, accum_out=total).then_inc(diag_summed, 1)
                if first:
                    act.wait_ge(diag_summed, 1)
                    nc.scalar.mul(diag_neg_shift[:, :], total, -1.0 / (2 * BAND)).then_inc(diag_shift_set, 1)
                    act.wait_ge(diag_shift_set, 1)
                nc.scalar.activation(diag(1, shape), src, ACT.Square, bias=diag_neg_shift[:, :], accum_out=squares).then_inc(diag_summed, 1)

            def pair_diag_sums(p, first=False):
                if not first:
                    act.wait_ge(diag_summed, 2 * p)
                    act.sem_inc(act_passed, 1)
                act.wait_ge(bands_made, 2 * p + 2)
                act.sem_inc(act_passed, 1)
                two = z[:, bass.ds(2 * p, 2), :].rearrange("c a q -> c (a q)")
                diag_sums(at(two, DIAG * BAND, [[PIX, 2], [1, BAND]]), [[BAND, 2], [1, BAND]], p, first)

            def keep_odd_pair(p):
                for k in range(2):
                    act.wait_ge(rows_split, p * 2 + k - 1)
                    keep_odd(p * 2 + k, k)

            keep_odd_pair(2)
            pair_diag_sums(0, True)
            with act.Fori(3, PAIRS) as p:
                keep_odd_pair(p)
                pair_diag_sums(p - 2)
            pair_diag_sums(PAIRS - 2)
            for i in range(2):
                n = IMAGES - 2 + i
                act.wait_ge(bands_made, n + 1)
                act.wait_ge(diag_summed, 2 * (PAIRS - 1 + i))
                diag_sums(z[:, n, DIAG * BAND:PIX], [[1, BAND]], PAIRS - 1 + i)

            def norm_bands(n):
                zb = zslot(n)
                for b in range(BANDS):
                    ins = nc.scalar.activation(zb[:, b * BAND:(b + 1) * BAND], zb[:, b * BAND:(b + 1) * BAND],
                                               ACT.Relu, bias=bn1[:, 5, b:b + 1], scale=bn1[:, 4, b:b + 1])
                ins.then_inc(bands_normed, 1)

            def split_r(n, k):
                act.wait_ge(r_made, n + 1)
                act.sem_inc(act_passed, 1)
                nc.scalar.activation(inner(r_hi[k]), rows(zslot(n)), ACT.Identity).then_inc(r_hi_set, 1)

            act.wait_ge(var1_ready, 1)
            nc.scalar.sqrt(bn1[:, 1, :], bn1[:, 0, :]).then_inc(sd1_ready, 1)
            act.wait_ge(bn1_ready, 1)
            norm_bands(0)
            split_r(0, 0)
            norm_bands(1)
            split_r(1, 1)

            def keep_y(count, dst, src, s):
                act.wait_ge(conv_done, count)
                nc.scalar.activation(dst, src, ACT.Identity, scale=sgn[:, :], accum_out=s).then_inc(y_kept, 1)

            def square_y(src, s):
                nc.scalar.activation(src, src, ACT.Square, bias=neg_shift[:, :], scale=sgn[:, :], accum_out=s).then_inc(squares_summed, 1)

            def image(n, k, first=False):
                norm_bands(n + 2)
                keep_y(n + 1, slot(n), conv_ps[:, k, :], y_sum[:, bass.ds(n, 1)])
                split_x(n + 2, k)
                if first:
                    act.wait_ge(y_kept, 1)
                    nc.scalar.mul(neg_shift[:, :], y_sum[:, 0:1], -1.0 / PIX).then_inc(shift_set, 1)
                    act.wait_ge(shift_set, 1)
                square_y(conv_ps[:, k, :], y_sq[:, bass.ds(n, 1)])
                split_r(n + 2, k)

            act.wait_ge(sgn_ready, 1)
            image(0, 0, True)
            image(1, 1)
            with act.Fori(1, WHOLE // 2) as p:
                for k in range(2):
                    image(p * 2 + k, k)
            part = WHOLE
            for n in range(WHOLE, IMAGES):
                if n + 2 < IMAGES:
                    norm_bands(n + 2)
                for row, nrows, bank in PIECES[n]:
                    src = conv_banks[piece_bank(n, bank)][:, 0:nrows * W]
                    keep_y(part + 1, slot(n)[:, row * W:(row + nrows) * W], src, y_sum[:, part:part + 1])
                    square_y(src, y_sq[:, part:part + 1])
                    part += 1
                if n + 2 < IMAGES:
                    split_x(n + 2, n % 2)
                    split_r(n + 2, n % 2)

            act.wait_ge(var3_ready, 1)
            nc.scalar.sqrt(sd3[:, :], var3[:, :]).then_inc(sd3_ready, 1)
            act.wait_ge(bn3_ready, 1)
            act.wait_ge(med_made, 1)
            for b in range(2):
                half = z[:, 0, b * BANK:(b + 1) * BANK]
                nc.scalar.activation(half, half, ACT.Relu, bias=shift3[:, :], scale=scale3[:, :]).then_inc(half_normed, 1)

            def norm_median(n):
                act.wait_ge(med_made, n + 1)
                nc.scalar.activation(zslot(n), zslot(n), ACT.Relu, bias=shift3[:, :], scale=scale3[:, :]).then_inc(med_normed, 1)

            def map_x1(n):
                nc.scalar.activation(slot(n), slot(n), ACT.Identity, bias=shift3_bias2[:, :], scale=scale3[:, :]).then_inc(x1_by_act, 1)

            for n in range(1, 4):
                norm_median(n)
            for n in range(4 - ACT_SHARE, 4):
                map_x1(n)
            with act.Fori(1, IMAGES // 4) as g:
                for k in range(4):
                    norm_median(g * 4 + k)
                    if k >= 4 - ACT_SHARE:
                        map_x1(g * 4 + k)

        @block.vector
        def _(dve):
            count = [0]

            def after(base, back=0):
                dve.wait_ge(dve_done, base + (count[0] - back))

            def step(ins):
                count[0] += 1
                ins.then_inc(dve_done, 1)

            def chain(*args, op):
                step(op(*args))
                after(0)

            V = nc.vector
            V.memset(zeros[:, :], 0.0).then_inc(warm, 1)

            def analyse_rows(k, pair0=0, pairs=BH):
                even = at(one_ps[:, k, :], pair0 * 2 * W, [[2 * W, pairs], [2, BW], [1, 2]])
                odd = at(odd_rows[k], pair0 * W, [[W, pairs], [2, BW], [1, 2]])
                for off, op in ((0, ALU.add), (HALF, ALU.subtract)):
                    ins = V.tensor_tensor(at(row_pairs[k], off + pair0 * BW, [[BW, pairs], [1, BW], [BAND, 2]]), even, odd, op)
                return ins

            def band_stats(p, bands):
                dve.wait_ge(bands_made, 2 * p + 2)
                two = z[:, bass.ds(2 * p, 2), :].rearrange("c a q -> c (a q)")
                for b in bands:
                    V.bn_stats(stats1[:, b, bass.ds(p, 1), :].rearrange("c a s -> c (a s)"),
                               at(two, b * BAND, [[PIX, 2], [1, BAND]]))

            def image_stats(n, group):
                dve.wait_ge(bands_made, n + 1)
                for b in range(DIAG):
                    step(V.bn_stats(stats1[:, b, group, :], z[:, n, b * BAND:(b + 1) * BAND]))

            dve.wait_ge(odd_half_kept, 1)
            analyse_rows(0, 0, BH // 2).then_inc(rows_half_split, 1)
            dve.wait_ge(odd_kept, 1)
            analyse_rows(0, BH // 2, BH // 2).then_inc(rows_split, 1)
            dve.wait_ge(odd_kept, 2)
            analyse_rows(1).then_inc(rows_split, 1)
            def split_w3(half):
                c = half * TAPS * CH
                V.tensor_tensor(w3_lo[:, c:c + TAPS * CH], w3_raw[half], fl(w3_hi[:, c:c + TAPS * CH]),
                                ALU.subtract).then_inc(w3_ready, 1)

            dve.wait_ge(x_hi_set, 1)
            V.tensor_tensor(inner(x_lo[0]), rows(slot(0)), fl(inner(x_hi[0])), ALU.subtract).then_inc(x_split, 1)
            dve.wait_ge(bands_made, 1)
            dve.wait_ge(odd_kept, 3)
            analyse_rows(0).then_inc(rows_split, 1)
            dve.wait_ge(w3_hi_set, 1)
            split_w3(1)
            dve.wait_ge(bands_made, 2)
            dve.wait_ge(odd_kept, 4)
            analyse_rows(1).then_inc(rows_split, 1)
            def rows_and_stats(p):
                for k in range(2):
                    n = p * 2 + k
                    dve.wait_ge(bands_made, n - 1)
                    dve.wait_ge(odd_kept, n + 1)
                    analyse_rows(k).then_inc(rows_split, 1)
                    band_stats(p - 2, ((0, 1), (2,))[k])

            dve.wait_ge(vec_in, 16)
            chain(sgn[:, :], g3, 0.0, None, ALU.is_lt, op=V.tensor_scalar)
            V.tensor_scalar(sgn[:, :], sgn[:, :], -2.0, 1.0, ALU.mult, ALU.add).then_inc(sgn_ready, 1)
            step(V.tensor_scalar(half_bn1[:, 0:1], g1, 0.5, None, ALU.mult))
            step(V.tensor_scalar(half_bn1[:, 1:2], b1, 0.5, None, ALU.mult))

            rows_and_stats(2)
            with dve.Fori(3, PAIRS) as p:
                rows_and_stats(p)
            band_stats(PAIRS - 2, range(DIAG))
            image_stats(IMAGES - 2, PAIRS - 1)
            image_stats(IMAGES - 1, PAIRS)
            after(0)

            def aggregate(b):
                step(V.bn_aggr(mv1[:, b, :], stats1[:, b, :, :].rearrange("c a s -> c (a s)")))

            aggregate(0)
            N1 = IMAGES * BAND
            dve.wait_ge(diag_summed, 2 * (PAIRS + 1))
            step(V.reduce_sum(diag_total[:, :], diag_sum[:, :], axis=mybir.AxisListType.X))
            step(V.reduce_sum(diag_sq_total[:, :], diag_sq[:, :], axis=mybir.AxisListType.X))
            aggregate(1)
            after(0, 2)
            step(V.tensor_scalar(diag_off[:, :], diag_total[:, :], 1.0 / N1, diag_neg_shift[:, :], ALU.mult, ALU.add))
            step(V.tensor_scalar(diag_neg_off[:, :], diag_total[:, :], -1.0 / N1, diag_neg_shift[:, :], ALU.mult, ALU.subtract))
            step(V.tensor_scalar(mv1[:, DIAG, 0:1], diag_total[:, :], 1.0 / N1, None, ALU.mult))
            after(0, 4)
            step(V.tensor_scalar(diag_sq_mean[:, :], diag_sq_total[:, :], 1.0 / N1, None, ALU.mult))
            aggregate(2)
            after(0, 1)
            step(V.scalar_tensor_tensor(mv1[:, DIAG, 1:2], diag_off[:, :], diag_neg_off[:, :], diag_sq_mean[:, :], ALU.mult, ALU.add))
            after(0)
            V.tensor_scalar(bn1[:, 0, :], mv1[:, :, 1], EPS, None, ALU.add).then_inc(var1_ready, 1)

            var_eps, sd, rstd, t, scale1, shift1 = (bn1[:, k, :] for k in range(6))
            dve.wait_ge(var1_ready, 1)
            dve.wait_ge(sd1_ready, 1)
            chain(rstd, sd, op=V.reciprocal)
            step(V.tensor_tensor(t, rstd, rstd, ALU.mult))
            after(0)
            step(V.tensor_tensor(t, t, var_eps, ALU.mult))
            step(V.tensor_scalar(rstd, rstd, half_bn1[:, 0:1], None, ALU.mult))
            after(0, 1)
            chain(t, t, -0.5, 1.5, ALU.mult, ALU.add, op=V.tensor_scalar)
            chain(scale1, rstd, t, ALU.mult, op=V.tensor_tensor)
            chain(t, mv1[:, :, 0], scale1, ALU.mult, op=V.tensor_tensor)
            V.tensor_scalar(shift1, t, -1.0, half_bn1[:, 1:2], ALU.mult, ALU.add).then_inc(bn1_ready, 1)
            dve.wait_ge(w3_hi_set, 2)
            split_w3(0)
            for t in (col_lo, col_mid, col_hi):
                step(V.memset(at(t, 0, [[PITCH, H + 1]]), LOW))

            def prepare(n, k):
                zb = zslot(n)
                a_h = at(zb, 0, [[BAND, 2], [1, BAND]])
                v_d = at(zb, HALF, [[BAND, 2], [1, BAND]])
                dve.wait_ge(bands_normed, n + 1)
                dve.wait_ge(w3_ready, 2)
                step(V.tensor_tensor(at(syn[:, :], 0, [[HALF, 2], [2, BAND]]), a_h, v_d, ALU.add))
                step(V.tensor_tensor(at(syn[:, :], 1, [[HALF, 2], [2, BAND]]), a_h, v_d, ALU.subtract))
                after(0)
                low, high = rows(syn[:, 0:HALF]), rows(syn[:, HALF:PIX])
                step(V.tensor_tensor(even_rows(zb), low, high, ALU.add))
                V.tensor_tensor(other_rows(zb), low, high, ALU.subtract).then_inc(r_made, 1)
                dve.wait_ge(r_hi_set, n + 1)
                V.tensor_tensor(inner(r_lo[k]), rows(zb), fl(inner(r_hi[k])), ALU.subtract).then_inc(r_split, 1)

            for n in range(2):
                prepare(n, n)
            after(0)

            def median(n, base, kept, pair0=0, pairs=BH, step=step):
                r0, nr = 2 * pair0, 2 * pairs
                top = y[:, bass.ds(n * (ROWS * W) + r0 * W, (nr + 2) * W)]
                res = z[:, bass.ds(n, 1), :].rearrange("p a q -> p (a q)")
                dve.wait_ge(y_kept, kept)
                even = at(top, W, [[2 * W, pairs], [1, W]])
                odd = at(top, 2 * W, [[2 * W, pairs], [1, W]])
                third = at(top, 0, [[2 * W, pairs], [3 * W, 2], [1, W]])

                def sorted_rows(off):
                    return at(tmp1, off, [[W, pairs], [1, W]])

                def twice(off):
                    return at(tmp1, off, [[W, pairs], [0, 2], [1, W]])

                def cols(t):
                    return at(t, r0 * PITCH + 1, [[2 * PITCH, pairs], [PITCH, 2], [1, W]])

                step(V.tensor_tensor(sorted_rows(0), even, odd, ALU.min))
                step(V.tensor_tensor(sorted_rows(HALF), even, odd, ALU.max))
                after(base, 1)
                step(V.tensor_tensor(cols(col_mid), twice(0), third, ALU.max))
                step(V.tensor_tensor(cols(col_lo), twice(0), third, ALU.min))
                after(base, 2)
                step(V.tensor_tensor(cols(col_hi), twice(HALF), third, ALU.max))
                after(base, 2)
                step(V.tensor_tensor(cols(col_mid), twice(HALF), cols(col_mid), ALU.min))

                def pair(t, k):
                    return at(t, r0 * PITCH + 1 + k, [[PITCH, nr], [2, BW]])

                def outer(t):
                    return at(t, r0 * PITCH, [[PITCH, nr], [2, BW], [3, 2]])

                def both(off):
                    return at(tmp1, off, [[BW, nr], [1, BW], [0, 2]])

                def padded(t):
                    return at(t, r0 * PITCH + 1, [[PITCH, nr], [2, BW], [1, 2]])

                def body(t):
                    return at(t, r0 * PITCH + 1, [[PITCH, nr], [1, W]])

                p1 = at(tmp1, 0, [[BW, nr], [1, BW]])
                p2 = at(tmp1, HALF, [[BW, nr], [1, BW]])
                dense3 = at(tmp2, 0, [[W, nr], [2, BW], [1, 2]])
                dense = at(tmp2, 0, [[W, nr], [1, W]])
                after(base, 1)
                step(V.tensor_tensor(p1, pair(col_lo, 0), pair(col_lo, 1), ALU.max))
                after(base, 1)
                step(V.tensor_tensor(p2, pair(col_hi, 0), pair(col_hi, 1), ALU.min))
                after(base, 1)
                step(V.tensor_tensor(dense3, both(0), outer(col_lo), ALU.max))
                after(base)
                step(V.tensor_tensor(padded(col_lo), both(HALF), outer(col_hi), ALU.min))
                after(base, 1)
                step(V.tensor_tensor(p1, pair(col_mid, 0), pair(col_mid, 1), ALU.min))
                after(base, 1)
                step(V.tensor_tensor(p2, pair(col_mid, 0), pair(col_mid, 1), ALU.max))
                after(base)
                step(V.tensor_tensor(padded(col_hi), both(HALF), outer(col_mid), ALU.min))
                after(base)
                step(V.tensor_tensor(padded(col_hi), both(0), padded(col_hi), ALU.max))
                step(V.tensor_tensor(body(col_mid), dense, body(col_lo), ALU.min))
                after(base)
                step(V.tensor_tensor(dense, dense, body(col_lo), ALU.max))
                after(base)
                step(V.tensor_tensor(dense, dense, body(col_hi), ALU.min))
                after(base)
                return V.tensor_tensor(at(res, r0 * W, [[W, nr], [1, W]]), dense, body(col_mid), ALU.max)

            dve.wait_ge(sgn_ready, 1)
            step(V.tensor_tensor(abs_g3[:, :], g3, sgn[:, :], ALU.mult))
            step(V.tensor_scalar(neg_abs_g3[:, :], g3, sgn[:, :], -1.0, ALU.mult, ALU.mult))
            step(V.tensor_tensor(signed_b[:, :], cb3, sgn[:, :], ALU.mult))
            step(V.tensor_tensor(beta_bias2[:, :], b3, cb2, ALU.add))

            MED_STEPS = 17
            dve.wait_ge(pads_set, 1)
            start = count[0]
            with dve.Fori(0, WHOLE) as n:
                count[0] = 0
                median(n, n * MED_STEPS + start, n + 1).then_inc(med_made, 1)
                assert count[0] == MED_STEPS
                dve.wait_ge(med_made, n + 1)
            count[0] = start + MED_STEPS * WHOLE

            def by_pieces(n, first_part):
                found, done = [], 0
                for i, (row, nrows, _) in enumerate(PIECES[n]):
                    upto = BH if row + nrows == H else (row + nrows) // 2 - 1
                    found.append((n, done, upto - done, first_part + i + 1))
                    done = upto
                return found

            def medians(pieces, step=step):
                for n, pair0, pairs, parts in pieces:
                    ins = median(n, 0, parts, pair0, pairs, step)
                    if pair0 + pairs == BH:
                        ins.then_inc(med_made, 1)
                        dve.wait_ge(med_made, n + 1)
                    else:
                        step(ins)
                        after(0)

            todo = [piece for n in range(WHOLE, IMAGES) for piece in by_pieces(n, parts_before(n))]
            medians(todo[:-2])

            def second_batch_norm():
                dve.wait_ge(squares_summed, PARTS_ALL)
                N = IMAGES * PIX
                step(V.reduce_sum(y_total[:, :], y_sum[:, :], axis=mybir.AxisListType.X))
                step(V.reduce_sum(sq_total[:, :], y_sq[:, :], axis=mybir.AxisListType.X))
                after(0, 1)
                step(V.tensor_scalar(off3[:, :], y_total[:, :], 1.0 / N, neg_shift[:, :], ALU.mult, ALU.add))
                step(V.tensor_scalar(neg_off3[:, :], y_total[:, :], -1.0 / N, neg_shift[:, :], ALU.mult, ALU.subtract))
                after(0, 2)
                step(V.tensor_scalar(sq_eps3[:, :], sq_total[:, :], 1.0 / N, EPS, ALU.mult, ALU.add))
                step(V.tensor_scalar(mean3[:, :], y_total[:, :], 1.0 / N, None, ALU.mult))
                after(0, 1)
                V.scalar_tensor_tensor(var3[:, :], off3[:, :], neg_off3[:, :], sq_eps3[:, :], ALU.mult, ALU.add).then_inc(var3_ready, 1)
                after(0)
                chain(mid3[:, :], mean3[:, :], signed_b[:, :], signed_b[:, :], ALU.add, ALU.subtract, op=V.tensor_scalar)
                dve.wait_ge(sd3_ready, 1)
                chain(r3[:, :], sd3[:, :], op=V.reciprocal)
                dve.wait_ge(var3_ready, 1)
                chain(newton3[:, :], r3[:, :], r3[:, :], var3[:, :], ALU.mult, ALU.mult, op=V.scalar_tensor_tensor)
                chain(newton3[:, :], newton3[:, :], -0.5, 1.5, ALU.mult, ALU.add, op=V.tensor_scalar)
                step(V.scalar_tensor_tensor(neg_scale3[:, :], r3[:, :], neg_abs_g3[:, :], newton3[:, :], ALU.mult, ALU.mult))
                step(V.scalar_tensor_tensor(scale3[:, :], r3[:, :], abs_g3[:, :], newton3[:, :], ALU.mult, ALU.mult))
                after(0, 1)
                step(V.scalar_tensor_tensor(shift3[:, :], mid3[:, :], neg_scale3[:, :], b3, ALU.mult, ALU.add))
                V.scalar_tensor_tensor(shift3_bias2[:, :], mid3[:, :], neg_scale3[:, :], beta_bias2[:, :], ALU.mult, ALU.add).then_inc(bn3_ready, 1)

            def finish(n, first=0, count=PIX, part=0):
                g, k = divmod(n, 4)
                if k >= 4 - ACT_SHARE:
                    dve.wait_ge(x1_by_act, g * ACT_SHARE + k + 1 - (4 - ACT_SHARE))
                else:
                    dve.wait_ge(x1_by_pool, g * (4 - ACT_SHARE) + k + 1)
                dve.wait_ge(mix_done, n + 1 + part)
                v = slot(n)[:, first:first + count]
                V.scalar_tensor_tensor(v, v, cb2, conv_ps[:, n % 2, first:first + count], ALU.max, ALU.add).then_inc(out_ready, 1)

            place = {BN3_AT: second_batch_norm}
            for n, instruction in enumerate(FINISH_AT):
                place[instruction] = lambda n=n: finish(n)
            done = [0]

            def step_and_more(ins):
                step(ins)
                done[0] += 1
                if done[0] in place:
                    place.pop(done[0])()

            medians(todo[-2:], step_and_more)
            assert not place

            for n in range(len(FINISH_AT), IMAGES - 1):
                finish(n)
            for part in range(2):
                finish(IMAGES - 1, part * HALF, HALF, part)


def kernel(**inputs):
    import numpy as np
    import concourse.bacc as bacc
    from concourse.bass_utils import run_bass_kernel_spmd

    nc = bacc.Bacc("TRN2", target_bir_lowering=False, num_devices=1)
    w3 = np.asarray(inputs["L0_conv_convW_w"])
    o, i = w3.shape[:2]
    half = i // 2
    w3_t = w3.reshape(o, 2, half, 9).transpose(2, 1, 3, 0).reshape(half, 18, o)
    arrays = {
        "x": inputs["x"],
        "w1_t": np.asarray(inputs["L0_conv_conv_w"]).T,
        "w3_t": w3_t,
        "w2_t": np.asarray(inputs["L1_conv_W"]).T,
        "vectors": np.stack([np.asarray(inputs[k]) for k in (
            "L0_conv_bn_gamma", "L0_conv_bn_beta", "L0_conv_convW_b", "L0_conv_bnW_gamma", "L0_conv_bnW_beta", "L1_conv_b")], axis=1),
    }
    arrays = {k: np.ascontiguousarray(v) for k, v in arrays.items()}
    aps = [nc.dram_tensor(k, v.shape, mybir.dt.from_np(v.dtype), kind="ExternalInput").ap() for k, v in arrays.items()]
    shape = arrays["x"].shape
    out = nc.dram_tensor("out", shape, mybir.dt.float32, kind="ExternalOutput").ap()
    wavelet_conv_median_kernel(nc, *aps, out)
    r = run_bass_kernel_spmd(nc, [arrays], core_ids=[0])
    return r.results[0]["out"]
```
